# Optimizing a Trainium2 kernel written in Bass

```python
import numpy as np
import jax
import jax.numpy as jnp

def _softmax(x, axis=-1):
    return jax.nn.softmax(x, axis=axis)

def _gelu(x):
    return jax.nn.gelu(x, approximate=True)

def _silu(x):
    return jax.nn.silu(x)

def _sigmoid(x):
    return jax.nn.sigmoid(x)

def _layernorm(x, axis=-1, eps=1e-05):
    m = jnp.mean(x, axis=axis, keepdims=True)
    v = jnp.var(x, axis=axis, keepdims=True)
    return (x - m) / jnp.sqrt(v + eps)

def _scatter_add(tgt, idx, src, axis=0):
    return tgt.at[idx].add(src)

def _segment_sum(src, seg, n):
    return jax.ops.segment_sum(src, seg, n)
kernel_name = 'mk_xattn_seq_d1_seqx_r4_95ed9b'

def setup_inputs(seed: int=0):
    np.random.seed(seed)
    _w = jnp.asarray

    def _rec_inputs():
        import jax
        import jax.numpy as jnp
        _rk = jax.random.key(seed)
        x = 7.22e-05 + 1 * jax.random.normal(jax.random.fold_in(_rk, 1), (4, 512, 512), jnp.float32)
        _lenS = 512 - jax.random.randint(jax.random.fold_in(_rk, 7), (4,), 0, max(1, 512 // 4) + 1, jnp.int32)
        _lenS2 = 512 - jax.random.randint(jax.random.fold_in(_rk, 8), (4,), 0, max(1, 512 // 4) + 1, jnp.int32)
        _ctx_2048P = jax.random.normal(jax.random.fold_in(_rk, 11), (4, 16, 512), jnp.float32)
        _ctx_2048c = jax.random.dirichlet(jax.random.fold_in(_rk, 511), 0.3 * jnp.ones((16,), jnp.float32), (4, 512))
        _ctx_2048t = jnp.einsum('bsk,bkd->bsd', _ctx_2048c, _ctx_2048P)
        _ctx_2048t = _ctx_2048t * jax.lax.rsqrt(jnp.mean(jnp.square(_ctx_2048t)) + 1e-12) * 0.953939
        ctx_2048 = 2.81802e-05 + 1.00001 * (_ctx_2048t + 0.3 * jax.random.normal(jax.random.fold_in(_rk, 611), (4, 512, 512), jnp.float32))
        _validS = jnp.arange(512)[None, :] < _lenS[:, None]
        _validS2 = jnp.arange(512)[None, :] < _lenS2[:, None]
        _causal = jnp.tril(jnp.ones((512, 512), dtype=bool))
        mask_BxS2_bf1 = jnp.ones((4, 512), dtype=bool)
        return (x, ctx_2048, mask_BxS2_bf1)
    x, ctx_2048, mask_BxS2_bf1 = _rec_inputs()

    def _L0_xattn_setup():
        import jax, jax.numpy as jnp
        import numpy as np
        D = 512
        H = 16
        HD = D // H
        INNER = 4 * D
        EPS = 1e-05

        def layer_norm(x, w, b):
            mu = jnp.mean(x, axis=-1, keepdims=True)
            var = jnp.mean(jnp.square(x - mu), axis=-1, keepdims=True)
            return (x - mu) * jax.lax.rsqrt(var + EPS) * w + b
        key = jax.random.key(seed)
        ks = jax.random.split(key, 12)
        B, LQ, LK = (4, 256, 512)
        std = 0.02
        inp = {'hidden_states': jax.random.normal(ks[0], (B, LQ, D), jnp.float32), 'encoder_hidden_states': jax.random.normal(ks[1], (B, LK, D), jnp.float32), 'encoder_attention_mask': jnp.ones((B, LK), dtype=bool), 'ln1_w': jnp.ones((D,), jnp.float32), 'ln1_b': jnp.zeros((D,), jnp.float32), 'q_w': jax.random.normal(ks[2], (D, D), jnp.float32) * std, 'q_b': jnp.zeros((D,), jnp.float32), 'k_w': jax.random.normal(ks[3], (D, D), jnp.float32) * std, 'k_b': jnp.zeros((D,), jnp.float32), 'v_w': jax.random.normal(ks[4], (D, D), jnp.float32) * std, 'v_b': jnp.zeros((D,), jnp.float32), 'cproj_w': jax.random.normal(ks[5], (D, D), jnp.float32) * std, 'cproj_b': jnp.zeros((D,), jnp.float32), 'ln2_w': jnp.ones((D,), jnp.float32), 'ln2_b': jnp.zeros((D,), jnp.float32), 'fc_w': jax.random.normal(ks[6], (D, INNER), jnp.float32) * std, 'fc_b': jnp.zeros((INNER,), jnp.float32), 'proj_w': jax.random.normal(ks[7], (INNER, D), jnp.float32) * std, 'proj_b': jnp.zeros((D,), jnp.float32)}
        return inp
    _L0_xattn_all = _L0_xattn_setup()
    _L0_xattn_in = {k: v for k, v in _L0_xattn_all.items() if k in ('ln1_w', 'ln1_b', 'q_w', 'q_b', 'k_w', 'k_b', 'v_w', 'v_b', 'cproj_w', 'cproj_b', 'ln2_w', 'ln2_b', 'fc_w', 'fc_b', 'proj_w', 'proj_b')}
    del _L0_xattn_all
    return {'x': x, 'ctx_2048': ctx_2048, 'mask_BxS2_bf1': mask_BxS2_bf1, 'L0_xattn_ln1_w': _L0_xattn_in['ln1_w'], 'L0_xattn_ln1_b': _L0_xattn_in['ln1_b'], 'L0_xattn_q_w': _L0_xattn_in['q_w'], 'L0_xattn_q_b': _L0_xattn_in['q_b'], 'L0_xattn_k_w': _L0_xattn_in['k_w'], 'L0_xattn_k_b': _L0_xattn_in['k_b'], 'L0_xattn_v_w': _L0_xattn_in['v_w'], 'L0_xattn_v_b': _L0_xattn_in['v_b'], 'L0_xattn_cproj_w': _L0_xattn_in['cproj_w'], 'L0_xattn_cproj_b': _L0_xattn_in['cproj_b'], 'L0_xattn_ln2_w': _L0_xattn_in['ln2_w'], 'L0_xattn_ln2_b': _L0_xattn_in['ln2_b'], 'L0_xattn_fc_w': _L0_xattn_in['fc_w'], 'L0_xattn_fc_b': _L0_xattn_in['fc_b'], 'L0_xattn_proj_w': _L0_xattn_in['proj_w'], 'L0_xattn_proj_b': _L0_xattn_in['proj_b']}

def reference(x, ctx_2048, mask_BxS2_bf1, L0_xattn_ln1_w, L0_xattn_ln1_b, L0_xattn_q_w, L0_xattn_q_b, L0_xattn_k_w, L0_xattn_k_b, L0_xattn_v_w, L0_xattn_v_b, L0_xattn_cproj_w, L0_xattn_cproj_b, L0_xattn_ln2_w, L0_xattn_ln2_b, L0_xattn_fc_w, L0_xattn_fc_b, L0_xattn_proj_w, L0_xattn_proj_b):
    import jax
    import jax.numpy as jnp

    def _L0_xattn_ref(hidden_states, encoder_hidden_states, encoder_attention_mask, ln1_w, ln1_b, q_w, q_b, k_w, k_b, v_w, v_b, cproj_w, cproj_b, ln2_w, ln2_b, fc_w, fc_b, proj_w, proj_b):
        import jax, jax.numpy as jnp
        import numpy as np
        D = 512
        H = 16
        HD = D // H
        INNER = 4 * D
        EPS = 1e-05

        def layer_norm(x, w, b):
            mu = jnp.mean(x, axis=-1, keepdims=True)
            var = jnp.mean(jnp.square(x - mu), axis=-1, keepdims=True)
            return (x - mu) * jax.lax.rsqrt(var + EPS) * w + b
        B, LQ, _ = hidden_states.shape
        LK = encoder_hidden_states.shape[1]
        residual = hidden_states
        x = layer_norm(hidden_states, ln1_w, ln1_b)
        q = (x @ q_w + q_b).reshape(B, LQ, H, HD).transpose(0, 2, 1, 3)
        k = (encoder_hidden_states @ k_w + k_b).reshape(B, LK, H, HD).transpose(0, 2, 1, 3)
        v = (encoder_hidden_states @ v_w + v_b).reshape(B, LK, H, HD).transpose(0, 2, 1, 3)
        scale = 1.0 / np.sqrt(HD).astype(np.float32)
        scores = jnp.einsum('bhqd,bhkd->bhqk', q, k) * scale
        mask = encoder_attention_mask[:, None, None, :]
        mask_value = jnp.finfo(scores.dtype).min
        scores = jnp.where(mask, scores, mask_value)
        attn = jax.nn.softmax(scores, axis=-1)
        out = jnp.einsum('bhqk,bhkd->bhqd', attn, v)
        out = out.transpose(0, 2, 1, 3).reshape(B, LQ, D)
        out = out @ cproj_w + cproj_b
        hidden = out + residual
        residual = hidden
        y = layer_norm(hidden, ln2_w, ln2_b)
        y = jax.nn.gelu(y @ fc_w + fc_b, approximate=True)
        y = y @ proj_w + proj_b
        return residual + y
    x = _L0_xattn_ref(x, ctx_2048, mask_BxS2_bf1, L0_xattn_ln1_w, L0_xattn_ln1_b, L0_xattn_q_w, L0_xattn_q_b, L0_xattn_k_w, L0_xattn_k_b, L0_xattn_v_w, L0_xattn_v_b, L0_xattn_cproj_w, L0_xattn_cproj_b, L0_xattn_ln2_w, L0_xattn_ln2_b, L0_xattn_fc_w, L0_xattn_fc_b, L0_xattn_proj_w, L0_xattn_proj_b)
    return x

_drawn_inputs = setup_inputs


def setup_inputs(seed=0):
    import zlib

    import numpy as np

    out = dict(_drawn_inputs(seed))
    spreads = {'L0_xattn_ln1_w': (1.0, 0.6),
     'L0_xattn_ln1_b': (0.0, 0.8),
     'L0_xattn_q_b': (0.0, 0.8),
     'L0_xattn_k_b': (0.0, 0.8),
     'L0_xattn_v_b': (0.0, 0.1),
     'L0_xattn_cproj_b': (0.0, 0.1),
     'L0_xattn_ln2_w': (1.0, 0.2),
     'L0_xattn_ln2_b': (0.0, 0.342),
     'L0_xattn_fc_b': (0.0, 0.1),
     'L0_xattn_proj_b': (0.0, 0.1)}
    factors = {'L0_xattn_q_w': 7.391, 'L0_xattn_k_w': 7.323}
    for name, (base, spread) in spreads.items():
        noise = np.random.default_rng([zlib.crc32(name.encode()), seed]).standard_normal(out[name].shape)
        drawn = base * np.exp(spread * noise) if base else spread * noise
        out[name] = jnp.asarray(drawn.astype(out[name].dtype))
    for name, factor in factors.items():
        out[name] = (out[name] * factor).astype(out[name].dtype)
    return out
```

```python
import concourse.bass as bass
from concourse import mybir
from contextlib import ExitStack


def cross_attention_block(nc: bass.Bass, x, ctxT, mask, vecs, q_w, k_w, v_w, c_w, c_b, fc_w, pj_w, pj_b, out):
    F32 = mybir.dt.float32
    R = mybir.dt.float32r
    U8 = mybir.dt.uint8
    ALU = mybir.AluOpType
    ACT = mybir.ActivationFunctionType
    AX = mybir.AxisListType

    B, T, D, H = 4, 512, 512, 16
    SCALE = 1.0 / float(32 ** 0.5)
    EPS = 1e-5
    NS = 16
    NF = 16

    ctx = ExitStack()
    progs = {e: [] for e in ("sync", "scalar", "vector", "gpsimd", "tensor")}
    sems, counts = {}, {}

    def op(eng, sem, fn, *waits):
        if sem is not None:
            if sem not in sems:
                sems[sem] = ctx.enter_context(nc.semaphore("s_" + sem))
                counts[sem] = 0
            counts[sem] += 16 if sem.startswith("d_") else 1
        progs[eng].append((fn, [w for w in waits if w is not None], sem))
        return (sem, counts[sem]) if sem is not None else None

    def flush(name, eng):
        met = {}
        for fn, waits, sem in progs[name]:
            for s, v in waits:
                if met.get(s, 0) < v:
                    eng.wait_ge(sems[s], v)
                    met[s] = v
            ins = fn(eng)
            if sem is not None:
                ins.then_inc(sems[sem], 16 if sem.startswith("d_") else 1)

    with ctx:
        def sb(name, shape, dt):
            return ctx.enter_context(nc.sbuf_tensor(name, shape, dt))

        def phased(*kinds):
            made = []
            for n, (name, shape, dt) in enumerate(kinds):
                if n == len(kinds) - 1:
                    made.append(sb(name, shape, dt))
                else:
                    with nc.sbuf_tensor(name, shape, dt) as t:
                        made.append(t)
            return made

        BIG = sb("BIG", [128, 24576], R)
        WK, KP_, WK2 = phased(("WK", [128, 8192], R), ("Pt", [128, 8, 2, 512], F32), ("SLX", [128, 8192], R))
        RAWY, YT0 = phased(("RAWY", [128, 2, 4, 512], F32), ("YT0", [128, 2, 4, 512], R))
        with nc.sbuf_tensor("V", [128, 16, 512], F32) as V:
            pass
        YT1 = sb("YT1", [128, 2, 4, 512], R)
        HR = sb("HR", [128, 2, 2, 512], R)
        RW = sb("RW", [128, 2, 1024], F32)
        R0 = sb("R0", [128, 4, 512], F32)
        R1 = sb("R1", [128, 4, 512], F32)
        R2 = sb("R2", [128, 4, 512], F32)
        ident = sb("ident", [128, 128], F32)
        ones = sb("ones", [128, 32], F32)
        cbt = sb("cbt", [128, 512], F32)
        cols = sb("cols", [128, 28 + NF], F32)
        vec = cols[:, 0:28].rearrange("p (v k) -> p v k", k=4)
        fcb = cols[:, 28:28 + NF]
        st = sb("st", [128, 4, 6], F32)
        mv = sb("mv", [128, 2, 4, 2], F32)
        rs = sb("rs", [128, 2, 4], F32)
        ve = sb("ve", [128, 2, 4], F32)
        mh = sb("mh", [128, 4], F32)
        mx = sb("mx", [128, 2, 16], F32)
        ng = sb("ng", [128, 16], F32)
        rc = sb("rc", [128, 16], F32)
        mT = sb("mT", [16, 128], R)

        WQH, WQL = BIG[:, 0:2048], None
        WV = [BIG[:, i * 2048:(i + 1) * 2048].rearrange("p (k n) -> p k n", k=4) for i in range(2)]
        WKq = [WK[:, i * 2048:(i + 1) * 2048].rearrange("p (k n) -> p k n", k=4) for i in range(4)]
        CT = [[BIG[:, 4096 + (2 * i + s) * 2048:4096 + (2 * i + s + 1) * 2048].rearrange("p (k n) -> p k n", k=4)
               for s in range(2)] for i in range(2)]
        XT = [[BIG[:, 12288 + (2 * i + s) * 2048:12288 + (2 * i + s + 1) * 2048].rearrange("p (k n) -> p k n", k=4)
               for s in range(2)] for i in range(2)]
        QK = [BIG[:, 20480 + i * 1024:20480 + (i + 1) * 1024].rearrange("p (s n) -> p s n", s=2) for i in range(4)]
        WC = [BIG[:, 20480 + i * 2048:20480 + (i + 1) * 2048].rearrange("p (k n) -> p k n", k=4) for i in range(2)]
        STK = [[BIG[:, 4096 + (2 * i + s) * 2048:4096 + (2 * i + s + 1) * 2048].rearrange("p (j n) -> p j n", j=4)
                for s in range(2)] for i in range(3)]
        AT = [BIG[:, 16384 + s * 2048:16384 + (s + 1) * 2048].rearrange("p (g n) -> p g n", g=4) for s in range(2)]
        Pt = KP_
        YT = [YT0, YT1]

        def slab(f):
            base, off = (WK2, f * 2048) if f < 4 else (BIG, (f - 4) * 2048)
            return [base[:, off + i * 512:off + (i + 1) * 512] for i in range(4)]

        ps = [ctx.enter_context(nc.psum_tensor(f"ps{i}", [128, 2, 512], F32)) for i in range(4)]

        def bank(i):
            return ps[i // 2][:, i % 2, :]

        qs = nc.dram_tensor("qs", (NS, 2, 32, 4, 512), F32, kind="Internal").ap()
        ks = nc.dram_tensor("ks", (NS, 2, 32, 4, 512), F32, kind="Internal").ap()
        hd = nc.dram_tensor("hd", (16, 128, 512), F32, kind="Internal").ap()
        mk = nc.dram_tensor("mk", (B, 512), F32, kind="Internal").ap()

        xv = x.rearrange("b (c p) n -> b p c n", p=128)
        cv = ctxT.rearrange("b (k p) n -> b p k n", p=128)
        ov = out.rearrange("b (c p) n -> (b c) p n", p=128)
        kp = lambda w: w.rearrange("(k p) n -> p k n", p=128)

        def c_ident(e):
            return e.memset(ident[:, :], 0.0)
        t = op("gpsimd", "cst", c_ident)
        t_id = op("gpsimd", "cst", lambda e: e.affine_select(
            out=ident[:, :], in_=ident[:, :], compare_op=ALU.not_equal, fill=1.0, base=0,
            pattern=[[-1, 128]], channel_multiplier=1), t)
        t_ones = op("gpsimd", "cst", lambda e: e.memset(ones[:, :], 1.0))

        t_mh = op("gpsimd", "cst", lambda e: e.memset(mh[:, :], -0.5))

        raw = [RAWY[:, 0], RAWY[:, 1], R0[:, :, :], R1[:, :, :]]
        raw_free = [[], [], [], []]
        turn = [0]

        def load_raw(src):
            i = turn[0] % 4
            turn[0] += 1
            tok = op("sync", f"d_raw{i}", lambda e: e.dma_start(raw[i], src), *raw_free[i])
            return i, tok

        t_vec = None
        ctxs, xs = {}, {}
        r_wv = load_raw(kp(v_w))
        ctxs[0] = load_raw(cv[0])
        t_vec = op("scalar", "d_vec", lambda e: e.dma_start(cols[:, :], vecs))
        r_wk = load_raw(kp(k_w))
        xs[0] = load_raw(xv[0])
        t_cb = op("sync", "d_cb", lambda e: e.dma_start(cbt[:, :], c_b.partition_broadcast(128)))

        m8 = R2[0:4, 0, 0:128].bitcast(U8)
        mf = R2[0:4, 1, :]
        t_m8 = op("sync", "d_m8", lambda e: e.dma_start(m8, mask))
        t = op("vector", "v_mf", lambda e: e.tensor_scalar(mf, m8, 1.0, None, ALU.subtract), t_m8)
        t = op("vector", "v_mf", lambda e: e.tensor_scalar(mf, mf, 2.0 ** 127, None, ALU.mult), t)
        t_mk = op("scalar", "d_mk", lambda e: e.dma_start(mk, mf), t)

        def split_raw(r, hi, lo, he, le, *free):
            i, tok = r
            if he == "scalar":
                th = op("scalar", "a_hi", lambda e: e.activation(hi, raw[i], ACT.Copy), tok, *free)
            else:
                th = op("vector", "v_hi", lambda e: e.tensor_copy(hi, raw[i]), tok, *free)
            tl = op(le, "v_lo" if le == "vector" else "g_lo", lambda e: e.tensor_tensor(
                lo, raw[i], hi.bitcast(F32), ALU.subtract), th, tok, *free)
            raw_free[i] = [tl]
            return [th, tl]

        pm = [0]
        bank_free = {i: [] for i in range(8)}

        def mm3(outp, a, b, first=True, last=True):
            def f(e):
                for n, (u, v) in enumerate(((a[0], b[0]), (a[1], b[0]), (a[0], b[1]))):
                    ins = e.matmul(outp, u, v, start=first and n == 0, stop=last and n == 2)
                return ins
            return f

        def mm_block(outp, a_of, b_of):
            def f(e):
                for k in range(4):
                    ins = mm3(outp, a_of(k), b_of(k), first=k == 0, last=k == 3)(e)
                return ins
            return f

        ct_done, xt_done, v_done = {}, {}, {}
        ct_free, xt_free = {0: [], 1: []}, {0: [], 1: []}
        full = [R2[:, i, :] for i in range(4)]
        full_free = [[t_mk], [t_mk], [], []]
        nfull = [0]

        def norm_stats(src, slot, tag, *waits):
            for c in range(4):
                t = op("vector", "v_bn", lambda e, c=c: e.bn_stats(st[:, c, :], src[:, c, :]), *waits)
            for c in range(4):
                t2 = op("vector", "v_ag", lambda e, c=c: e.bn_aggr(mv[:, slot, c, :], st[:, c, :]), t)
            t3 = op("vector", "v_ve", lambda e: e.tensor_scalar(
                ve[:, slot, :], mv[:, slot, :, 1], EPS, None, ALU.add), t2)
            return op("gpsimd", "g_rs", lambda e: e.tensor_tensor(
                rs[:, slot, :], ve[:, slot, :], mh[:, :], ALU.pow), t3, t_mh)

        def norm_apply(src, slot, tok):
            for c in range(4):
                t = op("vector", "v_nm", lambda e, c=c: e.tensor_scalar(
                    src[:, c, :], src[:, c, :], mv[:, slot, c, 0:1], rs[:, slot, c:c + 1],
                    ALU.subtract, ALU.mult), tok)
            return t

        def turn_k(src, k, bk, *waits):
            def f(e):
                for c in range(4):
                    ins = e.transpose(bank(bk)[:, c * 128:(c + 1) * 128], src[:, c, k * 128:(k + 1) * 128], ident[:, :])
                return ins
            return op("tensor", "p_tr", f, t_id, *waits)

        def affine_split(k, bk, tt, w, b, hi, lo, fb, free):
            tf = op("vector", "v_fu", lambda e: e.tensor_scalar(
                fb, bank(bk), vec[:, w, k:k + 1], vec[:, b, k:k + 1], ALU.mult, ALU.add), tt, t_vec, *free)
            th = op("scalar", "a_xh", lambda e: e.activation(hi, fb, ACT.Copy), tf)
            tl = op("gpsimd", "g_xl", lambda e: e.tensor_tensor(lo, fb, hi.bitcast(F32), ALU.subtract), th)
            return tf, th, tl

        def xt_part(b):
            i, tok = xs[b]
            t = norm_stats(raw[i], b % 2, "x", tok)
            tn = norm_apply(raw[i], b % 2, t)
            done = []
            for k in range(4):
                tt = turn_k(raw[i], k, k, tn, *bank_free[k])
                n = nfull[0] % 4
                nfull[0] += 1
                tf, th, tl = affine_split(k, k, tt, 0, 1, XT[b % 2][0][:, k, :], XT[b % 2][1][:, k, :], full[n],
                                          full_free[n] + xt_free[b % 2])
                full_free[n] = [tl]
                bank_free[k] = [tf]
                done += [th, tl]
            raw_free[i] = [tt]
            xt_done[b] = done[-2:]

        kq_free = [[], [], [], []]
        nkq = [0]
        nbk = [0]
        sc_done = {}

        def proj_T(b, g, wt, w_done, acts, a_done, bias, scr, which):
            bk = 4 + nbk[0] % 4
            nbk[0] += 1
            tm = op("tensor", "p_pj", mm_block(
                bank(bk), lambda k: [w[:, k, g * 128:(g + 1) * 128] for w in wt],
                lambda k: [a[:, k, :] for a in acts]), *w_done, *a_done, *bank_free[bk])
            n = nkq[0] % 4
            nkq[0] += 1
            dst = QK[n]
            th = op("scalar", "a_qh", lambda e: e.activation(
                dst[:, 0, :], bank(bk), ACT.Identity, bias=vec[:, bias, g:g + 1]), tm, t_vec, *kq_free[n])
            tl = op("vector", "v_ql", lambda e: e.scalar_tensor_tensor(
                out=dst[:, 1, :], in0=bank(bk), scalar=vec[:, bias, g:g + 1], in1=dst[:, 0, :].bitcast(F32),
                op0=ALU.add, op1=ALU.subtract), th, t_vec)
            bank_free[bk] = [tl]
            for h, tok in ((0, th), (1, tl)):
                td = op("sync", f"d_qk{n}", lambda e, h=h: e.dma_start(
                    scr[4 * b + g, h].rearrange("d j t -> j d t"), dst[:, h, :].bitcast(F32)), tok)
            kq_free[n] = [td]
            sc_done[(which, 4 * b + g)] = td
            return tm

        def proj_V(b, c):
            bk = 4 + nbk[0] % 4
            nbk[0] += 1
            tm = op("tensor", "p_pj", mm_block(
                bank(bk), lambda k: [a[:, k, c * 128:(c + 1) * 128] for a in CT[b % 2]],
                lambda k: [w[:, k, :] for w in WV]), *wv_done, *ct_done[b], *bank_free[bk])
            tv = op("scalar", "a_v", lambda e: e.activation(V[:, 4 * b + c, :], bank(bk), ACT.Copy), tm)
            bank_free[bk] = [tv]
            v_done[b] = tv
            return tm

        wv_done = split_raw(r_wv, WV[0], WV[1], "vector", "vector")
        ct_done[0] = split_raw(ctxs[0], CT[0][0], CT[0][1], "scalar", "gpsimd")
        r_wq = load_raw(kp(q_w))
        wk_done = split_raw(r_wk, WKq[0], WKq[1], "scalar", "gpsimd")
        ctxs[1] = load_raw(cv[1])
        xt_part(0)
        wq_done = split_raw(r_wq, WKq[2], WKq[3], "scalar", "gpsimd")
        xs[1] = load_raw(xv[1])
        for b in range(B):
            for c in range(4):
                tm = proj_V(b, c)
            for g in range(4):
                tm = proj_T(b, g, WKq[0:2], wk_done, CT[b % 2], ct_done[b], 3, ks, "k")
            ct_free[b % 2] = [tm]
            if b + 1 < B:
                ct_done[b + 1] = split_raw(ctxs[b + 1], CT[(b + 1) % 2][0], CT[(b + 1) % 2][1], "scalar", "gpsimd",
                                           *ct_free[(b + 1) % 2])
                if b + 2 < B:
                    ctxs[b + 2] = load_raw(cv[b + 2])
                xt_part(b + 1)
                if b + 2 < B:
                    xs[b + 2] = load_raw(xv[b + 2])
            for g in range(4):
                tm = proj_T(b, g, WKq[2:4], wq_done, XT[b % 2], xt_done[b], 2, qs, "q")
            xt_free[b % 2] = [tm]
        t_p0 = tm

        stk_free = {0: [ct_free[0][0]], 1: [ct_free[1][0]], 2: [xt_free[0][0]]}
        stk_done = {}
        t_row = {}

        def load_stack(s):
            n = s % 3
            Q_, K_ = STK[n]
            both = lambda scr: scr[s].rearrange("h d j t -> (h d) j t")
            if s < 3:
                t1 = op("vector", "v_one", lambda e: e.memset(Q_[96:98, :, :].bitcast(F32), 1.0), *stk_free[n])
                t1 = op("vector", "v_one", lambda e: e.memset(K_[96:98, :, :].bitcast(F32), 1.0), *stk_free[n])
                t_row[n] = t1
            w = [sc_done[("q", s)], sc_done[("k", s)], t_row[n], t_mk, *stk_free[n]]
            qd, kd = Q_.bitcast(F32), K_.bitcast(F32)
            for d, src in ((qd[0:64], both(qs)), (kd[32:96], both(ks)), (qd[64:96], qs[s, 0]), (kd[0:32], ks[s, 0]),
                           (kd[96:97], mk[s // 4:s // 4 + 1].rearrange("o (a t) -> o a t", a=1).broadcast_to([1, 4, 512]))):
                t = op("sync", f"d_st{n}", lambda e, d=d, src=src: e.dma_start(d, src), *w)
            stk_done[s] = t

        u_free = [list(bank_free[0]) + list(bank_free[1]), list(bank_free[2]) + list(bank_free[3]),
                  list(bank_free[4]) + list(bank_free[5])]
        nu = [0]
        mx_free = [[], []]
        mx_part = {}
        m_done = {}
        stk_p1 = {}

        def max_unit(s, n):
            hp, qc = n % 2, n // 2
            u = nu[0] % 3
            nu[0] += 1
            Q_, K_ = STK[s % 3]

            def f(e):
                for i in range(2):
                    j = 2 * hp + i
                    ins = e.matmul(ps[u][:, i, :], Q_[0:97, j, qc * 128:(qc + 1) * 128], K_[0:97, j, :],
                                   start=True, stop=True)
                return ins
            tm = op("tensor", "p_s1", f, stk_done[s], *u_free[u])
            mo = mx[:, s % 2, :].rearrange("p (j c) -> p j c", j=4)[:, 2 * hp:2 * hp + 2, qc]
            tv = op("vector", "v_mx", lambda e: e.tensor_reduce(mo, ps[u][:, :, :], AX.X, ALU.max), tm, *mx_free[s % 2])
            u_free[u] = [tv]
            mx_part[s] = tv

        mt_free = []

        def max_rows(s):
            tn = op("vector", "v_ng", lambda e: e.tensor_scalar(ng[:, :], mx[:, s % 2, :], -1.0, None, ALU.mult),
                    mx_part[s], *ng_free)
            mx_free[s % 2] = [tn]
            tp = op("tensor", "p_mt", lambda e: e.transpose(bank(7)[0:16, 0:128], ng[:, :], ident[:, :]), tn,
                    t_id, *bank_free[7])
            ng_free[:] = [tp]
            ta = op("scalar", "a_mt", lambda e: e.activation(mT[:, :], bank(7)[0:16, 0:128], ACT.Copy), tp, *mt_free)
            bank_free[7] = [ta]
            q97 = STK[s % 3][0].bitcast(F32)[97:98, :, :]
            td = op("sync", "d_m", lambda e: e.dma_start(q97, mT[:, :].bitcast(F32)), ta)
            mt_free[:] = [td]
            m_done[s] = td

        ng_free = []
        p_done, p_read = {}, {i: [] for i in range(8)}
        p_last = {}

        def exp_unit(s, kc, hp):
            u = nu[0] % 3
            nu[0] += 1
            Q_, K_ = STK[s % 3]

            def f(e):
                for i in range(2):
                    j = 2 * hp + i
                    ins = e.matmul(ps[u][:, i, :], K_[0:98, j, kc * 128:(kc + 1) * 128], Q_[0:98, j, :],
                                   start=True, stop=True)
                return ins
            tm = op("tensor", "p_s2", f, stk_done[s], m_done[s], *u_free[u])
            r = (2 * (4 * s + kc) + hp) % 8
            ta = op("scalar", "a_ex", lambda e: e.activation(Pt[:, r, :, :], ps[u][:, :, :], ACT.Exp, scale=SCALE),
                    tm, t_p0, *p_read[r])
            u_free[u] = [ta]
            p_read[r] = []
            p_done[(s, kc, hp)] = ta
            stk_free[s % 3] = [tm]

        acc_done, acc_free = {}, [[], []]

        def add_unit(s, kc, hp):
            r = (2 * (4 * s + kc) + hp) % 8
            acc = R0[:, 2 * hp:2 * hp + 2, :]
            if kc == 0:
                return
            a = Pt[:, (r - 2) % 8, :, :] if kc == 1 else acc
            w = [p_done[(s, kc, hp)], p_done[(s, kc - 1, hp)]]
            w += acc_free[hp] if kc == 1 else [acc_done[(s, hp)]]
            eng, sem = ("vector", "v_ac") if (kc, hp) == (3, 1) else ("gpsimd", "g_ac")
            t = op(eng, sem, lambda e: e.tensor_tensor(acc, a, Pt[:, r, :, :], ALU.add), *w)
            acc_done[(s, hp)] = t
            p_read[r].append(t)
            if kc == 1:
                p_read[(r - 2) % 8].append(t)

        pv_done = {}

        def pv(s, kc):
            b, g = divmod(s, 4)

            def f(e):
                for j in range(4):
                    r = (2 * (4 * s + kc) + j // 2) % 8
                    c = (4 * g + j) * 32
                    ins = e.matmul(bank(6)[32 * j:32 * j + 32, :], V[:, 4 * b + kc, c:c + 32], Pt[:, r, j % 2, :],
                                   start=kc == 0, stop=kc == 3)
                return ins
            w = list(bank_free[6]) if kc == 0 else []
            t = op("tensor", "p_pv", f, p_done[(s, kc, 0)], p_done[(s, kc, 1)], v_done[b], *w)
            for hp in range(2):
                p_read[(2 * (4 * s + kc) + hp) % 8].append(t)
            if kc == 3:
                ta = op("scalar", "a_pv", lambda e: e.activation(R1[:, 0, :], bank(6), ACT.Copy), t, *att_free)
                bank_free[6] = [ta]
                pv_done[s] = ta

        att_free = []
        at_free = []
        t1_free = []
        at_done = {}

        def finish(s):
            g = s % 4

            def f(e):
                for j in range(4):
                    ins = e.matmul(bank(7)[32 * j:32 * j + 32, :], ones[:, :], R0[:, j, :], start=True, stop=True)
                return ins
            ts = op("tensor", "p_sm", f, acc_done[(s, 0)], acc_done[(s, 1)], t_ones, *bank_free[7])
            acc_free[0], acc_free[1] = [ts], [ts]
            t = op("vector", "v_t1", lambda e: e.transpose(R1[:, 1, :], bank(7)), ts)
            bank_free[7] = [t]
            t = op("vector", "v_rc", lambda e: e.reciprocal(rc[:, :], R1[:, 1, 0:512:32]), t)
            t = op("vector", "v_t2", lambda e: e.transpose(
                R1[:, 2, :].rearrange("p (a b) -> p a b", b=32),
                rc[:, :].rearrange("p (a o) -> p a o", o=1).broadcast_to([128, 16, 32])), t)
            tm = op("vector", "v_at", lambda e: e.tensor_tensor(R1[:, 3, :], R1[:, 0, :], R1[:, 2, :], ALU.mult),
                    t, pv_done[s], *t1_free)
            att_free[:] = [tm]
            w = list(at_free) if g == 0 else []
            th = op("scalar", "a_ah", lambda e: e.activation(
                AT[0][:, g, :], R1[:, 3, :], ACT.Identity, bias=vec[:, 4, g:g + 1]), tm, *w)
            tl = op("vector", "v_al", lambda e: e.scalar_tensor_tensor(
                out=AT[1][:, g, :], in0=R1[:, 3, :], scalar=vec[:, 4, g:g + 1], in1=AT[0][:, g, :].bitcast(F32),
                op0=ALU.add, op1=ALU.subtract), th)
            t1_free[:] = [tl]
            at_done[s] = [th, tl]

        hd_done = {}
        xr_free = [list(full_free[i]) for i in range(4)]

        def x_plus_bias(b):
            toks = []
            for c in range(4):
                t = op("sync", f"d_xr{c}", lambda e, c=c: e.dma_start(R2[:, c, :], xv[b][:, c, :]), *xr_free[c])
                toks.append(op("gpsimd", "g_xc", lambda e, c=c: e.tensor_tensor(
                    R2[:, c, :], R2[:, c, :], cbt[:, :], ALU.add), t, t_cb))
            return toks

        def cproj(b, toks):
            for h in range(2):
                u = nu[0] % 3
                nu[0] += 1

                def f(e, h=h, u=u):
                    for i in range(2):
                        c = 2 * h + i
                        ins = mm_block(ps[u][:, i, :], lambda k: [a[:, k, c * 128:(c + 1) * 128] for a in AT],
                                       lambda k: [w[:, k, :] for w in WC])(e)
                    return ins
                tm = op("tensor", "p_cp", f, *wc_done, *at_done[4 * b + 3], *at_done[4 * b + 2], *u_free[u])
                for i in range(2):
                    c = 2 * h + i
                    tv = op("vector", "v_hd", lambda e, i=i, c=c, u=u: e.tensor_tensor(
                        R2[:, c, :], ps[u][:, i, :], R2[:, c, :], ALU.add), tm, toks[c])
                    td = op("sync", f"d_hd{c}", lambda e, c=c: e.dma_start(hd[4 * b + c], R2[:, c, :]), tv)
                    xr_free[c] = [td]
                    hd_done[4 * b + c] = td
                u_free[u] = [tv]
            at_free[:] = [tm]

        ti = op("sync", "d_wc", lambda e: e.dma_start(R0[:, :, :], kp(c_w)), *raw_free[2])
        load_stack(0)
        load_stack(1)
        load_stack(2)
        wfree = [kq_free[0][0], kq_free[1][0], kq_free[2][0], kq_free[3][0]]
        th = op("vector", "v_wc", lambda e: e.tensor_copy(WC[0], R0[:, :, :]), ti, *wfree)
        tl = op("vector", "v_wc", lambda e: e.scalar_tensor_tensor(
            out=WC[1], in0=R0[:, :, :], scalar=1.0, in1=WC[0].bitcast(F32), op0=ALU.mult, op1=ALU.subtract), th)
        wc_done = [tl]
        acc_free[0], acc_free[1] = [tl], [tl]
        att_free[:] = list(raw_free[3])
        at_free[:] = list(xt_free[1])
        bank_free[6] = list(bank_free[6])

        maxes = [(s, n) for s in range(NS) for n in range(8)]
        nm = [0]

        def next_max():
            if nm[0] < len(maxes):
                s, n = maxes[nm[0]]
                nm[0] += 1
                max_unit(s, n)
                if n == 7:
                    return s
            return None

        for _ in range(12):
            s = next_max()
            if s is not None:
                max_rows(s)
        late = None
        NI = 4 * NS
        xtoks = {}
        for i in range(NI + 4):
            s, kc = divmod(i, 4)
            if i < NI:
                if kc == 0 and s + 2 < NS and s >= 1:
                    load_stack(s + 2)
                for hp in range(2):
                    exp_unit(s, kc, hp)
                    r = next_max()
                    if late is not None:
                        max_rows(late)
                        late = None
                    if r is not None:
                        late = r
                if i >= 5 and i % 4 == 1:
                    finish(s - 1)
                for hp in range(2):
                    add_unit(s, kc, hp)
            if 1 <= i <= NI:
                pv(*divmod(i - 1, 4))
            if i > NI and i % 4 == 1:
                finish((i - 5) // 4)
            if i % 16 == 8 and i < NI:
                xtoks[i // 16] = x_plus_bias(i // 16)
            if i >= 19 and i % 16 == 3:
                cproj((i - 19) // 16, xtoks[(i - 19) // 16])

        t_v = ("p_pv", counts["p_pv"])
        t_pe1 = ("p_cp", counts["p_cp"])
        r0_free = [("p_sm", counts["p_sm"])]
        g_tmp = [R1[:, 0, :], R1[:, 1, :]]
        g_free = [[att_free[0]], [att_free[0]]]
        fu = [R1[:, 2, :], R1[:, 3, :]]
        fu_free = [[t1_free[0]], [t1_free[0]]]
        ty_free = [[t_pe1] , []]
        t_pb = op("sync", "d_pb", lambda e: e.dma_start(cbt[:, :], pj_b.partition_broadcast(128)),
                  ("g_xc", counts["g_xc"]))

        last_s = [("p_s2", counts["p_s2"]), ("p_cp", counts["p_cp"]), ("p_pv", counts["p_pv"]),
                  ("g_ac", counts["g_ac"]), ("v_ac", counts["v_ac"])]
        rw_free = [[t_v], [t_v]]
        slab_done = {}

        def load_slab(f):
            n = f % 2
            op("sync", f"d_w{n}", lambda e: e.dma_start(
                RW[:, n, 0:512].rearrange("p (k n) -> p k n", k=4), kp(fc_w)[:, :, f * 128:(f + 1) * 128]), *rw_free[n])
            t = op("sync", f"d_w{n}", lambda e: e.dma_start(RW[:, n, 512:1024], pj_w[f * 128:(f + 1) * 128, :]),
                   *rw_free[n])
            sl = slab(f)
            done = []
            for i in range(2):
                src = RW[:, n, 512 * i:512 * i + 512]
                th = op("vector", "v_sh", lambda e, i=i, src=src: e.tensor_copy(sl[2 * i], src), t, *last_s)
                tl = op("gpsimd", "g_sl", lambda e, i=i, src=src: e.tensor_tensor(
                    sl[2 * i + 1], src, sl[2 * i].bitcast(F32), ALU.subtract), th)
                done += [th, tl]
            rw_free[n] = [done[3]]
            slab_done[f] = done[2:]

        yt_done = {}

        def ln2(b):
            for c in range(4):
                t = op("sync", "d_h0", lambda e, c=c: e.dma_start(R0[:, c, :], hd[4 * b + c]),
                       hd_done[4 * b + c], *r0_free)
            ts = norm_stats(R0, b % 2, "y", t)
            return norm_apply(R0, b % 2, ts)

        def yt_k(b, k, tn):
            bk = 6 + k % 2
            Y = YT[b % 2]
            tt = turn_k(R0, k, bk, tn, *bank_free[bk])
            n = k % 2
            tf, th, tl = affine_split(k, bk, tt, 5, 6, Y[:, 0, k, :], Y[:, 1, k, :], fu[n],
                                      fu_free[n] + yt_free[b % 2])
            bank_free[bk] = [tf]
            fu_free[n] = [tl]
            yt_done[b] = [th, tl]
            if k == 3:
                r0_free[:] = [tt]

        yt_free = [list(raw_free[0]) + list(raw_free[1]), [t_v]]
        load_slab(0)
        tn = ln2(0)
        for k in range(4):
            yt_k(0, k, tn)
        load_slab(1)

        for i in range(3):
            for q in (2 * i, 2 * i + 1):
                bank_free[q] = list(u_free[i])
        h_done = {}
        h_free = [[t_v], [t_v]]
        hb_free = [list(xr_free[c]) for c in range(4)]
        hb_done = {}

        def fc(i):
            b, f = divmod(i, NF)
            bk = 4 + i % 2
            sl = slab(f)
            Y = YT[b % 2]
            tm = op("tensor", "p_fc", mm_block(
                bank(bk), lambda k: [sl[s][:, k * 128:(k + 1) * 128] for s in range(2)],
                lambda k: [Y[:, s, k, :] for s in range(2)]),
                *slab_done[f], *yt_done[b], *bank_free[bk])
            if f == NF - 1:
                yt_free[b % 2] = [tm]
            n = i % 2
            tg = op("scalar", "a_g", lambda e: e.activation(
                g_tmp[n], bank(bk), ACT.Gelu_apprx_tanh, bias=fcb[:, f:f + 1]), tm, *g_free[n])
            bank_free[bk] = [tg]
            th = op("vector", "v_hh", lambda e: e.tensor_copy(HR[:, n, 0, :], g_tmp[n]), tg, *h_free[n])
            tl = op("vector", "v_hl", lambda e: e.tensor_tensor(
                HR[:, n, 1, :], g_tmp[n], HR[:, n, 0, :].bitcast(F32), ALU.subtract), th)
            g_free[n] = [tl]
            h_done[i] = [tl]

        def pj(i):
            b, f = divmod(i, NF)
            n = i % 2
            sl = slab(f)
            w = []
            if f == 0:
                for c in range(4):
                    w += bank_free[c]

            for c in range(4):
                tm = op("tensor", "p_pr", mm3(
                    bank(c), [HR[:, n, s, c * 128:(c + 1) * 128] for s in range(2)], [sl[2], sl[3]],
                    first=f == 0, last=f == NF - 1), *h_done[i], *(bank_free[c] if f == 0 else []))
                if f == NF - 1:
                    to = op("vector", "v_o", lambda e, c=c: e.tensor_tensor(
                        R2[:, c, :], bank(c), R2[:, c, :], ALU.add), tm, hb_done[(b, c)])
                    bank_free[c] = [to]
                    td = op("sync", f"d_o{c}", lambda e, c=c: e.dma_start(ov[4 * b + c], R2[:, c, :]), to)
                    hb_free[c] = [td]
            h_free[n] = [tm]

        tn = None
        NI = B * NF
        for i in range(NI + 1):
            b, f = divmod(i, NF)
            if i < NI:
                if b == 0 and 1 <= f < NF - 1:
                    pass
                fc(i)
            if i >= 1:
                pj(i - 1)
            if b == 0 and f + 2 < NF:
                load_slab(f + 2)
            if i < NI:
                if f == 1:
                    for c in range(4):
                        t = op("sync", f"d_hb{c}", lambda e, c=c, b=b: e.dma_start(R2[:, c, :], hd[4 * b + c]),
                               *hb_free[c])
                        hb_done[(b, c)] = op("gpsimd", "g_hb", lambda e, c=c: e.tensor_tensor(
                            R2[:, c, :], R2[:, c, :], cbt[:, :], ALU.add), t, t_pb)
                if b + 1 < B:
                    if f == 3:
                        tn = ln2(b + 1)
                    if 6 <= f < 10:
                        yt_k(b + 1, f - 6, tn)
        for c in range(4):
            s, v = hb_free[c][0]
            progs["sync"].append((None, [(s, v)], None))

        def flush_all(name, eng):
            tail = [p for p in progs[name] if p[0] is None]
            progs[name] = [p for p in progs[name] if p[0] is not None]
            flush(name, eng)
            for _, waits, _ in tail:
                for s, v in waits:
                    eng.wait_ge(sems[s], v)

        block = ctx.enter_context(nc.Block())

        @block.sync
        def _(eng):
            flush_all("sync", eng)

        @block.scalar
        def _(eng):
            flush_all("scalar", eng)

        @block.gpsimd
        def _(eng):
            flush_all("gpsimd", eng)

        @block.vector
        def _(eng):
            flush_all("vector", eng)

        @block.tensor
        def _(eng):
            flush_all("tensor", eng)


_PRE = "L0_xattn_"
_COLS = ["ln1_w", "ln1_b", "q_b", "k_b", "v_b", "ln2_w", "ln2_b", "fc_b"]
_REST = ["q_w", "k_w", "v_w", "cproj_w", "cproj_b", "fc_w", "proj_w", "proj_b"]


def kernel(**inputs):
    import numpy as _np
    import concourse.bacc as _bacc
    from concourse import mybir as _mybir
    from concourse.bass_utils import run_bass_kernel_spmd as _run

    nc = _bacc.Bacc("TRN2", target_bir_lowering=False, num_devices=1)
    data = {"x": _np.asarray(inputs["x"]),
            "ctxT": _np.asarray(inputs["ctx_2048"]).transpose(0, 2, 1),
            "mask": _np.asarray(inputs["mask_BxS2_bf1"]).view(_np.uint8)}
    data["vecs"] = _np.concatenate([_np.asarray(inputs[_PRE + n]).reshape(-1, 128).T for n in _COLS], axis=1)
    for n in _REST:
        data[n] = _np.asarray(inputs[_PRE + n])
    arrays, args = {}, []
    for n, a in data.items():
        a = _np.ascontiguousarray(a)
        arrays[f"in_{n}"] = a
        args.append(nc.dram_tensor(f"in_{n}", a.shape, _mybir.dt.from_np(a.dtype), kind="ExternalInput").ap())
    args.append(nc.dram_tensor("out_0", (4, 512, 512), _mybir.dt.float32, kind="ExternalOutput").ap())
    cross_attention_block(nc, *args)
    r = _run(nc, [arrays], core_ids=[0])
    return r.results[0]["out_0"]
```

```python
import concourse.bass as bass
from concourse import mybir
from contextlib import ExitStack


def cross_attention_block(nc: bass.Bass, x, ctxT, mask, vecs, q_w, k_w, v_w, c_w, c_b, fc_w, pj_w, pj_b, out):
    F32 = mybir.dt.float32
    R = mybir.dt.float32r
    U8 = mybir.dt.uint8
    ALU = mybir.AluOpType
    ACT = mybir.ActivationFunctionType
    AX = mybir.AxisListType

    B, T, D, H = 4, 512, 512, 16
    SCALE = 1.0 / float(32 ** 0.5)
    EPS = 1e-5
    NS = 16
    NF = 16

    ctx = ExitStack()
    progs = {e: [] for e in ("sync", "scalar", "vector", "gpsimd", "tensor")}
    sems, counts = {}, {}

    def op(eng, sem, fn, *waits):
        if sem is not None:
            if sem not in sems:
                sems[sem] = ctx.enter_context(nc.semaphore("s_" + sem))
                counts[sem] = 0
            counts[sem] += 16 if sem.startswith("d_") else 1
        progs[eng].append((fn, [w for w in waits if w is not None], sem))
        return (sem, counts[sem]) if sem is not None else None

    def flush(name, eng):
        met = {}
        for fn, waits, sem in progs[name]:
            for s, v in waits:
                if met.get(s, 0) < v:
                    eng.wait_ge(sems[s], v)
                    met[s] = v
            ins = fn(eng)
            if sem is not None:
                ins.then_inc(sems[sem], 16 if sem.startswith("d_") else 1)

    with ctx:
        def sb(name, shape, dt):
            return ctx.enter_context(nc.sbuf_tensor(name, shape, dt))

        def phased(*kinds):
            made = []
            for n, (name, shape, dt) in enumerate(kinds):
                if n == len(kinds) - 1:
                    made.append(sb(name, shape, dt))
                else:
                    with nc.sbuf_tensor(name, shape, dt) as t:
                        made.append(t)
            return made

        BIG = sb("BIG", [128, 24576], R)
        with nc.sbuf_tensor("WK", [128, 8192], R) as WK:
            pass
        with nc.sbuf_tensor("Pt", [128, 6, 2, 512], F32) as Pt, nc.sbuf_tensor("HN", [128, 4, 512], F32) as HN:
            pass
        SLX = sb("SLX", [128, 8192], R)
        RAWY, YT0 = phased(("RAWY", [128, 2, 4, 512], F32), ("YT0", [128, 2, 4, 512], R))
        with nc.sbuf_tensor("V", [128, 16, 512], F32) as V:
            pass
        RW = sb("RW", [128, 2, 1024], F32)
        YT1 = sb("YT1", [128, 2, 4, 512], R)
        HR = sb("HR", [128, 2, 2, 512], R)
        R0 = sb("R0", [128, 4, 512], F32)
        R1 = sb("R1", [128, 4, 512], F32)
        R2 = sb("R2", [128, 4, 512], F32)
        FU = sb("FU", [128, 2, 512], F32)
        ident = sb("ident", [128, 128], F32)
        ones = sb("ones", [128, 32], F32)
        cbt = sb("cbt", [128, 512], F32)
        cols = sb("cols", [128, 28 + NF], F32)
        vec = cols[:, 0:28].rearrange("p (v k) -> p v k", k=4)
        fcb = cols[:, 28:28 + NF]
        st = sb("st", [128, 4, 6], F32)
        mv = sb("mv", [128, 2, 4, 2], F32)
        rs = sb("rs", [128, 2, 4], F32)
        ve = sb("ve", [128, 2, 4], F32)
        mh = sb("mh", [128, 4], F32)
        mx = sb("mx", [128, 2, 16], F32)
        ng = sb("ng", [128, 16], F32)
        rc = sb("rc", [128, 16], F32)
        mT = sb("mT", [16, 128], R)

        WV = [BIG[:, i * 2048:(i + 1) * 2048].rearrange("p (k n) -> p k n", k=4) for i in range(2)]
        WKq = [WK[:, i * 2048:(i + 1) * 2048].rearrange("p (k n) -> p k n", k=4) for i in range(4)]
        CT = [[BIG[:, 4096 + (2 * i + s) * 2048:4096 + (2 * i + s + 1) * 2048].rearrange("p (k n) -> p k n", k=4)
               for s in range(2)] for i in range(2)]
        XT = [[BIG[:, 12288 + (2 * i + s) * 2048:12288 + (2 * i + s + 1) * 2048].rearrange("p (k n) -> p k n", k=4)
               for s in range(2)] for i in range(2)]
        QK = [BIG[:, 20480 + i * 1024:20480 + (i + 1) * 1024].rearrange("p (s n) -> p s n", s=2) for i in range(4)]
        WC = [BIG[:, 20480 + i * 2048:20480 + (i + 1) * 2048].rearrange("p (k n) -> p k n", k=4) for i in range(2)]
        STK = [[BIG[:, 4096 * i + s * 2048:4096 * i + (s + 1) * 2048].rearrange("p (j n) -> p j n", j=4)
                for s in range(2)] for i in (1, 3, 2)]
        AT = [BIG[:, 16384 + s * 2048:16384 + (s + 1) * 2048].rearrange("p (g n) -> p g n", g=4) for s in range(2)]
        YT = [YT0, YT1]

        PLACE = [(BIG, 0), (BIG, 1), (BIG, 6), (BIG, 7), (BIG, 4), (BIG, 5), (SLX, 0), (SLX, 1), (BIG, 2), (BIG, 3),
                 (SLX, 2), (BIG, 8), (BIG, 9), (BIG, 10), (BIG, 11), (SLX, 3)]

        def slab(f):
            base, n = PLACE[f]
            off = 2048 * n
            return [base[:, off + i * 512:off + (i + 1) * 512] for i in range(4)]

        ps = [ctx.enter_context(nc.psum_tensor(f"ps{i}", [128, 2, 512], F32)) for i in range(4)]

        def bank(i):
            return ps[i // 2][:, i % 2, :]

        qs = nc.dram_tensor("qs", (NS, 2, 32, 4, 512), F32, kind="Internal").ap()
        ks = nc.dram_tensor("ks", (NS, 2, 32, 4, 512), F32, kind="Internal").ap()
        hd = nc.dram_tensor("hd", (16, 128, 512), F32, kind="Internal").ap()
        mk = nc.dram_tensor("mk", (B, 512), F32, kind="Internal").ap()

        xv = x.rearrange("b (c p) n -> b p c n", p=128)
        cv = ctxT.rearrange("b (k p) n -> b p k n", p=128)
        ov = out.rearrange("b (c p) n -> (b c) p n", p=128)
        kp = lambda w: w.rearrange("(k p) n -> p k n", p=128)

        def c_ident(e):
            return e.memset(ident[:, :], 0.0)
        t = op("gpsimd", "cst", c_ident)
        t_id = op("gpsimd", "cst", lambda e: e.affine_select(
            out=ident[:, :], in_=ident[:, :], compare_op=ALU.not_equal, fill=1.0, base=0,
            pattern=[[-1, 128]], channel_multiplier=1), t)
        t_ones = op("gpsimd", "cst", lambda e: e.memset(ones[:, :], 1.0))

        t_mh = op("gpsimd", "cst", lambda e: e.memset(mh[:, :], -0.5))

        raw = [RAWY[:, 0], RAWY[:, 1], R0[:, :, :], R1[:, :, :]]
        raw_free = [[], [], [], []]
        turn = [0]

        def load_raws(*srcs):
            at = [(turn[0] + n) % 4 for n in range(len(srcs))]
            turn[0] += len(srcs)
            toks = [[] for _ in srcs]
            for h in range(2):
                for n, (i, src) in enumerate(zip(at, srcs)):
                    toks[n].append(op("sync", f"d_raw{i}{h}", lambda e, h=h, i=i, src=src: e.dma_start(
                        raw[i][:, 2 * h:2 * h + 2, :], src[:, 2 * h:2 * h + 2, :]), *raw_free[i]))
            return list(zip(at, toks))

        def load_raw(src):
            return load_raws(src)[0]

        t_vec = None
        ctxs, xs = {}, {}
        r_wv, ctxs[0] = load_raws(kp(v_w), cv[0])
        t_vec = op("scalar", "d_vec", lambda e: e.dma_start(cols[:, :], vecs))
        r_wk = load_raw(kp(k_w))
        xs[0] = load_raw(xv[0])

        def split_raw(r, hi, lo, he, le, *free):
            i, toks = r
            done = []
            for h in range(2):
                rh, hh, lh = [v[:, 2 * h:2 * h + 2, :] for v in (raw[i], hi, lo)]
                eng = he[h % len(he)]
                if eng == "scalar":
                    th = op("scalar", "a_hi", lambda e, rh=rh, hh=hh: e.activation(hh, rh, ACT.Copy), toks[h], *free)
                else:
                    th = op("vector", "v_hi", lambda e, rh=rh, hh=hh: e.tensor_copy(hh, rh), toks[h], *free)
                eng = le[h % len(le)]
                tl = op(eng, "v_lo" if eng == "vector" else "g_lo",
                        lambda e, rh=rh, hh=hh, lh=lh: e.tensor_tensor(lh, rh, hh.bitcast(F32), ALU.subtract),
                        th, toks[h], *free)
                done.append([th, tl])
            raw_free[i] = [d[1] for d in done]
            return done

        pm = [0]
        bank_free = {i: [] for i in range(8)}

        def mm3(outp, a, b, first=True, last=True):
            def f(e):
                for n, (u, v) in enumerate(((a[0], b[0]), (a[1], b[0]), (a[0], b[1]))):
                    ins = e.matmul(outp, u, v, start=first and n == 0, stop=last and n == 2)
                return ins
            return f

        def mm_block(outp, a_of, b_of, ks=range(4)):
            def f(e):
                for k in ks:
                    ins = mm3(outp, a_of(k), b_of(k), first=k == 0, last=k == 3)(e)
                return ins
            return f

        def flat(toks):
            return [t for h in toks for t in h]

        ct_done, xt_done, v_done = {}, {}, {}
        ct_free, xt_free = {0: [], 1: []}, {0: [], 1: []}
        full = [R2[:, i, :] for i in range(4)]
        full_free = [[], [], [], []]
        nfull = [0]

        def norm_rs(slot, tok):
            for c in range(4):
                t = op("vector", "v_ag", lambda e, c=c: e.bn_aggr(mv[:, slot, c, :], st[:, c, :]), tok)
            t = op("vector", "v_ve", lambda e: e.tensor_scalar(
                ve[:, slot, :], mv[:, slot, :, 1], EPS, None, ALU.add), t)
            return op("gpsimd", "g_rs", lambda e: e.tensor_tensor(
                rs[:, slot, :], ve[:, slot, :], mh[:, :], ALU.pow), t, t_mh)

        def norm_one(src, slot, c, tok):
            return op("vector", "v_nm", lambda e: e.tensor_scalar(
                src[:, c, :], src[:, c, :], mv[:, slot, c, 0:1], rs[:, slot, c:c + 1],
                ALU.subtract, ALU.mult), tok)

        def turn_k(src, k, bk, *waits):
            def f(e):
                for c in range(4):
                    ins = e.transpose(bank(bk)[:, c * 128:(c + 1) * 128], src[:, c, k * 128:(k + 1) * 128], ident[:, :])
                return ins
            return op("tensor", "p_tr", f, t_id, *waits)

        def affine_split(k, bk, tt, w, b, hi, lo, fb, free):
            tf = op("vector", "v_fu", lambda e: e.tensor_scalar(
                fb, bank(bk), vec[:, w, k:k + 1], vec[:, b, k:k + 1], ALU.mult, ALU.add), tt, t_vec, *free)
            th = op("scalar", "a_xh", lambda e: e.activation(hi, fb, ACT.Copy), tf)
            tl = op("gpsimd", "g_xl", lambda e: e.tensor_tensor(lo, fb, hi.bitcast(F32), ALU.subtract), th)
            return tf, th, tl

        xn_done = {}

        def xn_part(b):
            i, toks = xs[b]
            for c in range(4):
                t = op("vector", "v_bn", lambda e, c=c: e.bn_stats(st[:, c, :], raw[i][:, c, :]), toks[c // 2])
            t = norm_rs(b % 2, t)
            for c in range(4):
                xn_done[b] = norm_one(raw[i], b % 2, c, t)

        def xt_part(b):
            i, _ = xs[b]
            done = []
            for k in range(4):
                tt = turn_k(raw[i], k, k, xn_done[b], *bank_free[k])
                n = nfull[0] % 4
                nfull[0] += 1
                tf, th, tl = affine_split(k, k, tt, 0, 1, XT[b % 2][0][:, k, :], XT[b % 2][1][:, k, :], full[n],
                                          full_free[n] + xt_free[b % 2])
                full_free[n] = [tl]
                bank_free[k] = [tf]
                done += [[th, tl]]
            raw_free[i] = [tt]
            xt_done[b] = [done[1], done[3]]

        kq_free = [[], [], [], []]
        nkq = [0]
        nbk = [0]
        sc_done = {}

        def proj_T(b, g, wt, w_done, acts, a_done, bias, scr, which):
            bk = next_bank()
            for h in range(2):
                tm = op("tensor", "p_pj", mm_block(
                    bank(bk), lambda k: [w[:, k, g * 128:(g + 1) * 128] for w in wt],
                    lambda k: [a[:, k, :] for a in acts], range(2 * h, 2 * h + 2)), *w_done[h], *a_done[h],
                    *(bank_free[bk] if h == 0 else []))
            n = nkq[0] % 4
            nkq[0] += 1
            dst = QK[n]
            th = op("scalar", "a_qh", lambda e: e.activation(
                dst[:, 0, :], bank(bk), ACT.Identity, bias=vec[:, bias, g:g + 1]), tm, t_vec, *kq_free[n])
            tl = op("vector", "v_ql", lambda e: e.scalar_tensor_tensor(
                out=dst[:, 1, :], in0=bank(bk), scalar=vec[:, bias, g:g + 1], in1=dst[:, 0, :].bitcast(F32),
                op0=ALU.add, op1=ALU.subtract), th, t_vec)
            bank_free[bk] = [tl]
            for h, tok in ((0, th), (1, tl)):
                td = op("sync", f"d_qk{n}", lambda e, h=h: e.dma_start(
                    scr[4 * b + g, h].rearrange("d j t -> j d t"), dst[:, h, :].bitcast(F32)), tok)
            kq_free[n] = [td]
            sc_done[(which, 4 * b + g)] = td
            return tm

        def proj_V(b, cs):
            bks = [next_bank() for _ in cs]
            for h in range(2):
                for c, bk in zip(cs, bks):
                    tm = op("tensor", "p_pj", mm_block(
                        bank(bk), lambda k, c=c: [a[:, k, c * 128:(c + 1) * 128] for a in CT[b % 2]],
                        lambda k: [w[:, k, :] for w in WV], range(2 * h, 2 * h + 2)), *wv_done[h], *ct_done[b][h],
                        *(bank_free[bk] if h == 0 else []))
                    if h == 1:
                        tv = op("scalar", "a_v", lambda e, c=c, bk=bk: e.activation(
                            V[:, 4 * b + c, :], bank(bk), ACT.Copy), tm)
                        bank_free[bk] = [tv]
            v_done[b] = tv

        mm_banks = [4, 5, 6, 7]

        def next_bank():
            nbk[0] += 1
            return mm_banks[nbk[0] % len(mm_banks)]

        wv_done = split_raw(r_wv, WV[0], WV[1], ["vector"], ["vector"])
        ct_done[0] = split_raw(ctxs[0], CT[0][0], CT[0][1], ["scalar"], ["vector", "gpsimd"])
        r_wq = load_raw(kp(q_w))
        wk_done = split_raw(r_wk, WKq[0], WKq[1], ["scalar"], ["gpsimd", "vector"])
        ctxs[1] = load_raw(cv[1])
        xn_part(0)
        m8 = R2[0:4, 0, 0:128].bitcast(U8)
        mf = R2[0:4, 1, :]
        t_m8 = op("sync", "d_m8", lambda e: e.dma_start(m8, mask))
        t = op("vector", "v_mf", lambda e: e.tensor_scalar(mf, m8, 1.0, None, ALU.subtract), t_m8)
        t = op("vector", "v_mf", lambda e: e.tensor_scalar(mf, mf, 2.0 ** 127, None, ALU.mult), t)
        t_mk = op("sync", "d_mk", lambda e: e.dma_start(mk, mf), t)
        t_cb = op("sync", "d_cb", lambda e: e.dma_start(cbt[:, :], c_b.partition_broadcast(128)))
        full_free[0] = [t_mk]
        full_free[1] = [t_mk]
        wq_done = split_raw(r_wq, WKq[2], WKq[3], ["vector", "scalar"], ["gpsimd"])
        xs[1] = load_raw(xv[1])

        stk_free, stk_done, t_row = {}, {}, {}

        def load_stack(s):
            n = s % 3
            Q_, K_ = STK[n]
            both = lambda scr: scr[s].rearrange("h d j t -> (h d) j t")
            if s < 3:
                op("vector", "v_one", lambda e: e.memset(Q_[96:98, :, :].bitcast(F32), 1.0), *stk_free[n])
                t_row[n] = op("vector", "v_one", lambda e: e.memset(K_[96:98, :, :].bitcast(F32), 1.0), *stk_free[n])
            w = [sc_done[("q", s)], sc_done[("k", s)], t_row[n], t_mk, *stk_free[n]]
            qd, kd = Q_.bitcast(F32), K_.bitcast(F32)
            for d, src in ((qd[0:64], both(qs)), (kd[32:96], both(ks)), (qd[64:96], qs[s, 0]), (kd[0:32], ks[s, 0]),
                           (kd[96:97], mk[s // 4:s // 4 + 1].rearrange("o (a t) -> o a t", a=1).broadcast_to([1, 4, 512]))):
                t = op("sync", f"d_st{n}", lambda e, d=d, src=src: e.dma_start(d, src), *w)
            stk_done[s] = t

        maxes = [(s, n) for s in range(NS) for n in range(8)]
        nm = [0]

        def next_max():
            if nm[0] < len(maxes):
                s, n = maxes[nm[0]]
                nm[0] += 1
                max_unit(s, n)
                if n == 7:
                    return s
            return None

        u_free = [[], [], []]
        nu = [0]
        mx_free = [[], []]
        mx_part = {}
        m_done = {}

        def max_unit(s, n):
            hp, qc = n % 2, n // 2
            u = nu[0] % 3
            nu[0] += 1
            Q_, K_ = STK[s % 3]

            def f(e):
                for i in range(2):
                    j = 2 * hp + i
                    ins = e.matmul(ps[u][:, i, :], Q_[0:97, j, qc * 128:(qc + 1) * 128], K_[0:97, j, :],
                                   start=True, stop=True)
                return ins
            tm = op("tensor", "p_s1", f, stk_done[s], *u_free[u])
            mo = mx[:, s % 2, :].rearrange("p (j c) -> p j c", j=4)[:, 2 * hp:2 * hp + 2, qc]
            tv = op("vector", "v_mx", lambda e: e.tensor_reduce(mo, ps[u][:, :, :], AX.X, ALU.max), tm, *mx_free[s % 2])
            u_free[u] = [tv]
            mx_part[s] = tv

        mt_free = []

        ng_free = []
        ng_done = {}

        def max_neg(s):
            tn = op("vector", "v_ng", lambda e: e.tensor_scalar(ng[:, :], mx[:, s % 2, :], -1.0, None, ALU.mult),
                    mx_part[s], *ng_free)
            mx_free[s % 2] = [tn]
            ng_done[s] = tn

        def max_rows(s):
            tn = ng_done[s]
            tp = op("tensor", "p_mt", lambda e: e.transpose(bank(7)[0:16, 0:128], ng[:, :], ident[:, :]), tn,
                    t_id, *bank_free[7])
            ng_free[:] = [tp]
            ta = op("scalar", "a_mt", lambda e: e.activation(mT[:, :], bank(7)[0:16, 0:128], ACT.Copy), tp, *mt_free)
            bank_free[7] = [ta]
            q97 = STK[s % 3][0].bitcast(F32)[97:98, :, :]
            td = op("sync", "d_m", lambda e: e.dma_start(q97, mT[:, :].bitcast(F32)), ta)
            mt_free[:] = [td]
            m_done[s] = td


        for b in range(B):
            if b == B - 1:
                u_free[2] = []
                stk_free[0] = ct_free[0]
                stk_free[1] = xt_free[0]
                load_stack(0)
                load_stack(1)
            if b == 0:
                proj_V(b, range(4))
            else:
                proj_V(b, range(2))
                proj_V(b, range(2, 4))
            if b + 1 < B and b > 0:
                xn_part(b + 1)
            for g in range(4):
                tm = proj_T(b, g, WKq[0:2], wk_done, CT[b % 2], ct_done[b], 3, ks, "k")
            ct_free[b % 2] = [tm]
            if b == 0:
                xt_part(0)
                xn_part(1)
            if b + 1 < B:
                ct_done[b + 1] = split_raw(ctxs[b + 1], CT[(b + 1) % 2][0], CT[(b + 1) % 2][1], ["scalar"],
                                           ["gpsimd"], *ct_free[(b + 1) % 2])
                if b + 2 < B:
                    ctxs[b + 2] = load_raw(cv[b + 2])
                if b > 0:
                    xt_part(b + 1)
                    if b + 2 < B:
                        xs[b + 2] = load_raw(xv[b + 2])
            if b == B - 1:
                u_free[0] = bank_free[0] + bank_free[1]
                u_free[1] = bank_free[2] + bank_free[3]
                u_free[2] = bank_free[4] + bank_free[5]
                mm_banks[:] = [6, 7]
                stk_free[2] = ct_free[1]
                load_stack(2)
            for g in range(4):
                if b == B - 1 and g == 3:
                    max_rows(0)
                tm = proj_T(b, g, WKq[2:4], wq_done, XT[b % 2], xt_done[b], 2, qs, "q")
                if b == 0 and g == 1:
                    xt_part(1)
                    xs[2] = load_raw(xv[2])
                if b == B - 1:
                    for _ in range(3):
                        r = next_max()
                        if r is not None:
                            max_neg(r)
            xt_free[b % 2] = [tm]
        t_p0 = tm

        p_done, p_read = {}, {i: [] for i in range(6)}
        p_last = {}

        def exp_unit(s, kc, hp):
            u = nu[0] % 3
            nu[0] += 1
            Q_, K_ = STK[s % 3]

            def f(e):
                for i in range(2):
                    j = 2 * hp + i
                    ins = e.matmul(ps[u][:, i, :], K_[0:98, j, kc * 128:(kc + 1) * 128], Q_[0:98, j, :],
                                   start=True, stop=True)
                return ins
            tm = op("tensor", "p_s2", f, stk_done[s], m_done[s], *u_free[u])
            r = (2 * (4 * s + kc) + hp) % 6
            ta = op("scalar", "a_ex", lambda e: e.activation(Pt[:, r, :, :], ps[u][:, :, :], ACT.Exp, scale=SCALE),
                    tm, t_p0, *p_read[r])
            u_free[u] = [ta]
            p_read[r] = []
            p_done[(s, kc, hp)] = ta
            stk_free[s % 3] = [tm]

        acc_done, acc_free = {}, [[], []]

        def add_unit(s, kc, hp):
            r = (2 * (4 * s + kc) + hp) % 6
            a, c = Pt[:, (r - 2) % 6, :, :], Pt[:, r, :, :]
            t = op("gpsimd", "g_ac", lambda e: e.tensor_tensor(R0[:, 2 * hp:2 * hp + 2, :], a, c, ALU.add),
                   p_done[(s, kc, hp)], p_done[(s, kc - 1, hp)], *acc_free[hp])
            acc_done[(s, kc, hp)] = t
            p_read[r].append(t)
            p_read[(r - 2) % 6].append(t)

        pv_done = {}

        def pv(s, kc):
            b, g = divmod(s, 4)

            def f(e):
                for j in range(4):
                    r = (2 * (4 * s + kc) + j // 2) % 6
                    c = (4 * g + j) * 32
                    ins = e.matmul(bank(6)[32 * j:32 * j + 32, :], V[:, 4 * b + kc, c:c + 32], Pt[:, r, j % 2, :],
                                   start=kc == 0, stop=kc == 3)
                return ins
            w = list(bank_free[6]) if kc == 0 else []
            t = op("tensor", "p_pv", f, p_done[(s, kc, 0)], p_done[(s, kc, 1)], v_done[b], *w)
            for hp in range(2):
                p_read[(2 * (4 * s + kc) + hp) % 6].append(t)
            if kc == 3:
                ta = op("scalar", "a_pv", lambda e: e.activation(R1[:, 0, :], bank(6), ACT.Copy), t, *att_free)
                bank_free[6] = [ta]
                pv_done[s] = ta

        att_free = []
        at_free = []
        t1_free = []
        at_done = {}

        at_tok = {}

        def sums(s, kc):
            def f(e):
                for j in range(4):
                    ins = e.matmul(bank(7)[32 * j:32 * j + 32, :], ones[:, :], R0[:, j, :], start=kc == 1, stop=kc == 3)
                return ins
            ts = op("tensor", "p_sm", f, acc_done[(s, kc, 0)], acc_done[(s, kc, 1)], t_ones,
                    *(bank_free[7] if kc == 1 else []))
            acc_free[0], acc_free[1] = [ts], [ts]
            at_tok[s] = ts

        def divide(s):
            t = op("vector", "v_t1", lambda e: e.transpose(R1[:, 1, :], bank(7)), at_tok[s])
            bank_free[7] = [t]
            t = op("vector", "v_rc", lambda e: e.reciprocal(rc[:, :], R1[:, 1, 0:512:32]), t)
            t = op("vector", "v_t2", lambda e: e.transpose(
                R1[:, 2, :].rearrange("p (a b) -> p a b", b=32),
                rc[:, :].rearrange("p (a o) -> p a o", o=1).broadcast_to([128, 16, 32])), t)
            tm = op("vector", "v_at", lambda e: e.tensor_tensor(R1[:, 3, :], R1[:, 0, :], R1[:, 2, :], ALU.mult),
                    t, pv_done[s], *t1_free)
            att_free[:] = [tm]
            at_tok[s] = tm

        def split_out(s):
            g = s % 4
            w = list(at_free) if g == 0 else []
            ta = R1[:, 3, :]
            t = op("scalar", "a_ab", lambda e: e.activation(ta, ta, ACT.Identity, bias=vec[:, 4, g:g + 1]), at_tok[s])
            th = op("scalar", "a_ah", lambda e: e.activation(AT[0][:, g, :], ta, ACT.Copy), t, *w)
            tl = op("gpsimd", "g_al", lambda e: e.tensor_tensor(
                AT[1][:, g, :], ta, AT[0][:, g, :].bitcast(F32), ALU.subtract), th, t)
            t1_free[:] = [tl]
            at_done[s] = [th, tl]

        hd_done = {}
        xr_free = [list(full_free[i]) for i in range(4)]

        def x_plus_bias(b):
            toks = []
            for c in range(4):
                t = op("sync", f"d_xr{c}", lambda e, c=c: e.dma_start(R2[:, c, :], xv[b][:, c, :]), *xr_free[c])
                toks.append(op("gpsimd", "g_xc", lambda e, c=c: e.tensor_tensor(
                    R2[:, c, :], R2[:, c, :], cbt[:, :], ALU.add), t, t_cb))
            return toks

        def cproj_tile(b, c, toks, outp, *waits):
            tm = op("tensor", "p_cp", mm_block(
                outp, lambda k: [a[:, k, c * 128:(c + 1) * 128] for a in AT], lambda k: [w[:, k, :] for w in WC]),
                *wc_done, *at_done[4 * b + 3], *at_done[4 * b + 2], *waits)
            tv = op("vector", "v_hd", lambda e: e.tensor_tensor(R2[:, c, :], outp, R2[:, c, :], ALU.add), tm, toks[c])
            td = op("sync", f"d_hd{c}", lambda e: e.dma_start(hd[4 * b + c], R2[:, c, :]), tv)
            xr_free[c] = [td]
            hd_done[4 * b + c] = td
            at_free[:] = [tm]
            return tv

        def cproj(b, toks):
            for h in range(2):
                u = nu[0] % 3
                nu[0] += 1
                for i in range(2):
                    tv = cproj_tile(b, 2 * h + i, toks, ps[u][:, i, :], *(u_free[u] if i == 0 else []))
                u_free[u] = [tv]

        ti = op("sync", "d_wc", lambda e: e.dma_start(R2[:, :, :], kp(c_w)), *[t for f in full_free for t in f])
        wfree = [f[0] for f in kq_free]
        wc_done = []

        def split_wc(k):
            th = op("scalar", "a_wc", lambda e: e.activation(WC[0][:, k, :], R2[:, k, :], ACT.Copy), ti, *wfree)
            tl = op("vector", "v_wc", lambda e: e.tensor_tensor(
                WC[1][:, k, :], R2[:, k, :], WC[0][:, k, :].bitcast(F32), ALU.subtract), th)
            wc_done.append(tl)
            xr_free[k] = [tl]

        acc_free[0], acc_free[1] = list(raw_free[2]), list(raw_free[2])
        att_free[:] = list(raw_free[3])
        at_free[:] = list(xt_free[1])

        rw_free = [[("p_pv", 0)], [("p_pv", 0)]]
        nslab = [0]
        slab_done = {}

        def load_slab(f, *waits):
            n = nslab[0] % 2
            nslab[0] += 1
            op("sync", f"d_w{n}", lambda e: e.dma_start(
                RW[:, n, 0:512].rearrange("p (k n) -> p k n", k=4), kp(fc_w)[:, :, f * 128:(f + 1) * 128]), *rw_free[n])
            t = op("sync", f"d_w{n}", lambda e: e.dma_start(RW[:, n, 512:1024], pj_w[f * 128:(f + 1) * 128, :]),
                   *rw_free[n])
            sl = slab(f)
            done = []
            for i in range(2):
                src = RW[:, n, 512 * i:512 * i + 512]
                th = op("vector", "v_sh", lambda e, i=i, src=src: e.tensor_copy(sl[2 * i], src), t, *waits)
                tl = op("gpsimd", "g_sl", lambda e, i=i, src=src: e.tensor_tensor(
                    sl[2 * i + 1], src, sl[2 * i].bitcast(F32), ALU.subtract), th)
                done += [th, tl]
            rw_free[n] = [done[3]]
            slab_done[f] = [done[2], done[3]]

        LN = [HN, R0, R0, R0]
        ln_free = {}
        ln_tok = {}
        yt_done, yt_free = {}, [raw_free[0] + raw_free[1], []]
        fu_free = [[], []]

        def ln2_load(b):
            for c in range(4):
                ln_tok[(b, c)] = op("sync", f"d_h{c}", lambda e, c=c: e.dma_start(LN[b][:, c, :], hd[4 * b + c]),
                                    hd_done[4 * b + c], *ln_free[b])

        def ln2_bn(b, c):
            ln_tok[(b, "bn")] = op("vector", "v_bn", lambda e: e.bn_stats(st[:, c, :], LN[b][:, c, :]), ln_tok[(b, c)])

        def ln2_rs(b):
            ln_tok[(b, "rs")] = norm_rs(b % 2, ln_tok[(b, "bn")])

        def ln2_norm(b, c):
            ln_tok[(b, "nm")] = norm_one(LN[b], b % 2, c, ln_tok[(b, "rs")])

        def yt_k(b, k, bk):
            Y = YT[b % 2]
            tt = turn_k(LN[b], k, bk, ln_tok[(b, "nm")], *bank_free[bk])
            n = k % 2
            tf, th, tl = affine_split(k, bk, tt, 5, 6, Y[:, 0, k, :], Y[:, 1, k, :], FU[:, n, :],
                                      fu_free[n] + yt_free[b % 2])
            bank_free[bk] = [tf]
            fu_free[n] = [tl]
            yt_done[b] = [th, tl]
            ln_free[b + 1] = [tt]

        h_done = {}
        h_free = [[], []]
        g_free = {}
        hb_done = {}

        def fc(i):
            b, f = divmod(i, NF)
            bk = 4 + i % 2
            sl = slab(f)
            Y = YT[b % 2]
            tm = op("tensor", "p_fc", mm_block(
                bank(bk), lambda k: [sl[s][:, k * 128:(k + 1) * 128] for s in range(2)],
                lambda k: [Y[:, s, k, :] for s in range(2)]),
                *slab_done[f], *yt_done[b], *bank_free[bk])
            if f == NF - 1:
                yt_free[b % 2] = [tm]
            n = i % 2
            early = i < 12
            g = HN[:, n, :] if early else R1[:, n, :]
            tg = op("scalar", "a_g", lambda e: e.activation(
                g, bank(bk), ACT.Gelu_apprx_tanh, bias=fcb[:, f:f + 1]), tm, *g_free[(early, n)])
            bank_free[bk] = [tg]
            th = op("vector", "v_hh", lambda e: e.tensor_copy(HR[:, n, 0, :], g), tg, *h_free[n])
            tl = op("vector", "v_hl", lambda e: e.tensor_tensor(
                HR[:, n, 1, :], g, HR[:, n, 0, :].bitcast(F32), ALU.subtract), th)
            g_free[(early, n)] = [tl]
            h_done[i] = [tl]

        def pj(i):
            b, f = divmod(i, NF)
            n = i % 2
            sl = slab(f)
            for c in range(4):
                tm = op("tensor", "p_pr", mm3(
                    bank(c), [HR[:, n, s, c * 128:(c + 1) * 128] for s in range(2)], [sl[2], sl[3]],
                    first=f == 0, last=f == NF - 1), *h_done[i], *(bank_free[c] if f == 0 else []))
                if f == NF - 1:
                    to = op("vector", "v_o", lambda e, c=c: e.tensor_tensor(
                        R2[:, c, :], bank(c), R2[:, c, :], ALU.add), tm, hb_done[(b, c)])
                    bank_free[c] = [to]
                    xr_free[c] = [op("sync", f"d_o{c}", lambda e, c=c: e.dma_start(ov[4 * b + c], R2[:, c, :]), to)]
            h_free[n] = [tm]

        NI = 4 * NS
        xtoks = {}
        late = []
        for i in range(NI):
            s, kc = divmod(i, 4)
            if kc == 0 and s >= 1 and s + 2 < NS:
                load_stack(s + 2)
            if i >= 5 and kc == 2:
                divide(s - 1)
            for hp in range(2):
                exp_unit(s, kc, hp)
                r = next_max()
                late = [(q, n - 1) for q, n in late]
                if late and late[0][1] == 0:
                    max_rows(late.pop(0)[0])
                if r is not None:
                    max_neg(r)
                    late.append((r, 2))
            if i >= 5 and kc == 1:
                sums(s - 1, 3)
            if kc == 3:
                sums(s, 1)
            if i >= 5 and kc == 3:
                split_out(s - 1)
            if kc % 2:
                for hp in range(2):
                    add_unit(s, kc, hp)
            if i >= 1:
                pv(*divmod(i - 1, 4))
            if 1 <= i <= 4:
                split_wc(i - 1)
            if i % 16 == 8:
                xtoks[i // 16] = x_plus_bias(i // 16)
            if i >= 20 and i % 16 == 4:
                cproj(i // 16 - 1, xtoks[i // 16 - 1])
            if i == 23:
                ln_free[0] = [t_p0]
                ln2_load(0)
            if 26 <= i < 30:
                ln2_bn(0, i - 26)
            if i == 30:
                ln2_rs(0)
            if 31 <= i < 39 and i % 2:
                ln2_norm(0, (i - 31) // 2)
            if 42 <= i < 58 and i % 4 == 2:
                yt_k(0, (i - 42) // 4, 7)
            if i in (49, 52):
                if i == 49:
                    rw_free = [[("p_pv", counts["p_pv"])]] * 2
                load_slab((i - 49) // 3, t_p0)
            if i in (57, 59):
                load_slab((i - 57) // 2 + 2, ("p_s2", s14))
            if i == 55:
                s14 = counts["p_s2"]
        s15 = counts["p_s2"]
        pv(NS - 1, 3)
        t_v = ("p_pv", counts["p_pv"])
        for q in range(3):
            bank_free[2 * q] = list(u_free[q])
            bank_free[2 * q + 1] = list(u_free[q])
        yt_free[1] = [t_v]
        h_free = [[t_v], [t_v]]
        g_free = {(True, n): list(ln_free[1]) for n in range(2)}
        t_pb = op("sync", "d_pb", lambda e: e.dma_start(cbt[:, :], pj_b.partition_broadcast(128)),
                  ("g_xc", counts["g_xc"]))
        load_slab(4, ("p_s2", s15))
        load_slab(5, ("p_s2", s15))

        NJ = B * NF
        for i in range(NJ + 1):
            b, f = divmod(i, NF)
            if i < NJ:
                fc(i)
            if i == 0:
                sums(NS - 1, 3)
                divide(NS - 1)
                split_out(NS - 1)
                g_free[(False, 0)] = g_free[(False, 1)] = [att_free[0]]
                ln_free[1] = [("p_sm", counts["p_sm"])]
            if i >= 1:
                pj(i - 1)
            if 2 <= i < 6:
                bk = 6 + i % 2
                bank_free[bk] = [cproj_tile(3, i - 2, xtoks[3], bank(bk), *bank_free[bk])]
            if 1 <= i < 9:
                load_slab(i + 5, t_v, ("g_ac", counts["g_ac"]), 
                          *([("p_cp", counts["p_cp"])] if i >= 6 else []))
            if i == 9:
                load_slab(14, ("p_cp", counts["p_cp"]))
            if i == 13:
                load_slab(15, *g_free[(True, 0)], *g_free[(True, 1)])
            if i < NJ:
                if f == (8 if b == 0 else 3):
                    for c in range(4):
                        t = op("sync", f"d_hb{c}", lambda e, c=c, b=b: e.dma_start(R2[:, c, :], hd[4 * b + c]),
                               *xr_free[c])
                        hb_done[(b, c)] = op("gpsimd", "g_hb", lambda e, c=c: e.tensor_tensor(
                            R2[:, c, :], R2[:, c, :], cbt[:, :], ALU.add), t, t_pb)
                if b + 1 < B:
                    if f == 2:
                        ln2_load(b + 1)
                    if 3 <= f < 7:
                        ln2_bn(b + 1, f - 3)
                    if f == 6:
                        ln2_rs(b + 1)
                    if 7 <= f < 11:
                        ln2_norm(b + 1, f - 7)
                    if 11 <= f < 15:
                        yt_k(b + 1, f - 11, 6 + f % 2)
        for c in range(4):
            progs["sync"].append((None, list(xr_free[c]), None))

        def flush_all(name, eng):
            tail = [p for p in progs[name] if p[0] is None]
            progs[name] = [p for p in progs[name] if p[0] is not None]
            flush(name, eng)
            for _, waits, _ in tail:
                for s, v in waits:
                    eng.wait_ge(sems[s], v)

        block = ctx.enter_context(nc.Block())

        @block.sync
        def _(eng):
            flush_all("sync", eng)

        @block.scalar
        def _(eng):
            flush_all("scalar", eng)

        @block.gpsimd
        def _(eng):
            flush_all("gpsimd", eng)

        @block.vector
        def _(eng):
            flush_all("vector", eng)

        @block.tensor
        def _(eng):
            flush_all("tensor", eng)


_PRE = "L0_xattn_"
_COLS = ["ln1_w", "ln1_b", "q_b", "k_b", "v_b", "ln2_w", "ln2_b", "fc_b"]
_REST = ["q_w", "k_w", "v_w", "cproj_w", "cproj_b", "fc_w", "proj_w", "proj_b"]


def kernel(**inputs):
    import numpy as _np
    import concourse.bacc as _bacc
    from concourse import mybir as _mybir
    from concourse.bass_utils import run_bass_kernel_spmd as _run

    nc = _bacc.Bacc("TRN2", target_bir_lowering=False, num_devices=1)
    data = {"x": _np.asarray(inputs["x"]),
            "ctxT": _np.asarray(inputs["ctx_2048"]).transpose(0, 2, 1),
            "mask": _np.asarray(inputs["mask_BxS2_bf1"]).view(_np.uint8)}
    data["vecs"] = _np.concatenate([_np.asarray(inputs[_PRE + n]).reshape(-1, 128).T for n in _COLS], axis=1)
    for n in _REST:
        data[n] = _np.asarray(inputs[_PRE + n])
    arrays, args = {}, []
    for n, a in data.items():
        a = _np.ascontiguousarray(a)
        arrays[f"in_{n}"] = a
        args.append(nc.dram_tensor(f"in_{n}", a.shape, _mybir.dt.from_np(a.dtype), kind="ExternalInput").ap())
    args.append(nc.dram_tensor("out_0", (4, 512, 512), _mybir.dt.float32, kind="ExternalOutput").ap())
    cross_attention_block(nc, *args)
    r = _run(nc, [arrays], core_ids=[0])
    return r.results[0]["out_0"]
```

```python
import concourse.bass as bass
from concourse import mybir
from contextlib import ExitStack


def cross_attention_block(nc: bass.Bass, x, ctxT, mask, vecs, q_w, k_w, v_w, c_w, c_b, fc_w, pj_w, pj_b, out):
    F32 = mybir.dt.float32
    R = mybir.dt.float32r
    U8 = mybir.dt.uint8
    ALU = mybir.AluOpType
    ACT = mybir.ActivationFunctionType
    AX = mybir.AxisListType

    B = 4
    SCALE = 1.0 / float(32 ** 0.5)
    EPS = 1e-5
    NS = 16
    NF = 16

    ctx = ExitStack()
    progs = {e: [] for e in ("sync", "scalar", "vector", "gpsimd", "tensor")}
    sems, counts = {}, {}

    def op(eng, sem, fn, *waits):
        if sem is not None:
            if sem not in sems:
                sems[sem] = ctx.enter_context(nc.semaphore("s_" + sem))
                counts[sem] = 0
            counts[sem] += 16 if sem.startswith("d_") else 1
        progs[eng].append((fn, [w for w in waits if w is not None], sem))
        return (sem, counts[sem]) if sem is not None else None

    def flush(name, eng):
        met = {}
        for fn, waits, sem in progs[name]:
            for s, v in waits:
                if met.get(s, 0) < v:
                    eng.wait_ge(sems[s], v)
                    met[s] = v
            ins = fn(eng)
            if sem is not None:
                ins.then_inc(sems[sem], 16 if sem.startswith("d_") else 1)

    with ctx:
        def sb(name, shape, dt):
            return ctx.enter_context(nc.sbuf_tensor(name, shape, dt))

        def phased(*kinds):
            made = []
            for n, (name, shape, dt) in enumerate(kinds):
                if n == len(kinds) - 1:
                    made.append(sb(name, shape, dt))
                else:
                    with nc.sbuf_tensor(name, shape, dt) as t:
                        made.append(t)
            return made

        BIG = sb("BIG", [128, 24576], R)
        with nc.sbuf_tensor("WK", [128, 8192], R) as WK:
            pass
        with nc.sbuf_tensor("Pt", [128, 6, 2, 512], F32) as Pt, nc.sbuf_tensor("HN", [128, 4, 512], F32) as HN:
            pass
        SLX = sb("SLX", [128, 8192], R)
        RAWY, YT0 = phased(("RAWY", [128, 2, 4, 512], F32), ("YT0", [128, 2, 4, 512], R))
        with nc.sbuf_tensor("V", [128, 16, 512], F32) as V:
            pass
        RW = sb("RW", [128, 2, 1024], F32)
        YT1 = sb("YT1", [128, 2, 4, 512], R)
        HR = sb("HR", [128, 2, 2, 512], R)
        R0 = sb("R0", [128, 4, 512], F32)
        R1 = sb("R1", [128, 4, 512], F32)
        R2 = sb("R2", [128, 4, 512], F32)
        FU = sb("FU", [128, 2, 512], F32)
        ident = sb("ident", [128, 128], F32)
        ones = sb("ones", [128, 32], F32)
        cbt = sb("cbt", [128, 512], F32)
        cols = sb("cols", [128, 28 + NF], F32)
        vec = cols[:, 0:28].rearrange("p (v k) -> p v k", k=4)
        fcb = cols[:, 28:28 + NF]
        st = sb("st", [128, 4, 6], F32)
        mv = sb("mv", [128, 2, 4, 2], F32)
        rs = sb("rs", [128, 2, 4], F32)
        ve = sb("ve", [128, 2, 4], F32)
        mh = sb("mh", [128, 4], F32)
        mx = sb("mx", [128, 2, 16], F32)
        rc = sb("rc", [128, 16], F32)
        mT = sb("mT", [16, 128], R)

        WV = [BIG[:, i * 2048:(i + 1) * 2048].rearrange("p (k n) -> p k n", k=4) for i in range(2)]
        WKq = [WK[:, i * 2048:(i + 1) * 2048].rearrange("p (k n) -> p k n", k=4) for i in range(4)]
        CT = [[BIG[:, 4096 + (2 * i + s) * 2048:4096 + (2 * i + s + 1) * 2048].rearrange("p (k n) -> p k n", k=4)
               for s in range(2)] for i in range(2)]
        XT = [[BIG[:, 12288 + (2 * i + s) * 2048:12288 + (2 * i + s + 1) * 2048].rearrange("p (k n) -> p k n", k=4)
               for s in range(2)] for i in range(2)]
        QK = [BIG[:, 20480 + i * 1024:20480 + (i + 1) * 1024].rearrange("p (s n) -> p s n", s=2) for i in range(4)]
        WC = [BIG[:, 20480 + i * 2048:20480 + (i + 1) * 2048].rearrange("p (k n) -> p k n", k=4) for i in range(2)]
        STK = [[BIG[:, 4096 * i + s * 2048:4096 * i + (s + 1) * 2048].rearrange("p (j n) -> p j n", j=4)
                for s in range(2)] for i in (1, 3, 2)]
        AT = [BIG[:, 16384 + s * 2048:16384 + (s + 1) * 2048].rearrange("p (g n) -> p g n", g=4) for s in range(2)]
        YT = [YT0, YT1]

        PLACE = [(BIG, 0), (BIG, 1), (BIG, 6), (BIG, 7), (BIG, 4), (BIG, 5), (SLX, 0), (SLX, 1), (BIG, 2), (BIG, 3),
                 (SLX, 2), (BIG, 8), (BIG, 9), (BIG, 10), (BIG, 11), (SLX, 3)]

        def slab(f):
            base, n = PLACE[f]
            off = 2048 * n
            return [base[:, off + i * 512:off + (i + 1) * 512] for i in range(4)]

        ps = [ctx.enter_context(nc.psum_tensor(f"ps{i}", [128, 2, 512], F32)) for i in range(4)]

        def bank(i):
            return ps[i // 2][:, i % 2, :]

        qs = nc.dram_tensor("qs", (NS, 2, 32, 4, 512), F32, kind="Internal").ap()
        ks = nc.dram_tensor("ks", (NS, 2, 32, 4, 512), F32, kind="Internal").ap()
        hd = nc.dram_tensor("hd", (16, 128, 512), F32, kind="Internal").ap()
        mk = nc.dram_tensor("mk", (B, 512), F32, kind="Internal").ap()

        on = nc.dram_tensor("on", (1, 512), F32, kind="Internal").ap()

        xv = x.rearrange("b (c p) n -> b p c n", p=128)
        cv = ctxT.rearrange("b (k p) n -> b p k n", p=128)
        ov = out.rearrange("b (c p) n -> (b c) p n", p=128)
        kp = lambda w: w.rearrange("(k p) n -> p k n", p=128)

        t = op("gpsimd", "cst", lambda e: e.memset(ident[:, :], 0.0))
        t_id = op("gpsimd", "cst", lambda e: e.affine_select(
            out=ident[:, :], in_=ident[:, :], compare_op=ALU.not_equal, fill=1.0, base=0,
            pattern=[[-1, 128]], channel_multiplier=1), t)
        t_ones = op("gpsimd", "cst", lambda e: e.memset(ones[:, :], 1.0))
        t_mh = op("gpsimd", "cst", lambda e: e.memset(mh[:, :], -0.5))

        raw = [RAWY[:, 0], RAWY[:, 1], R0[:, :, :], R1[:, :, :]]
        raw_free = [[], [], [], []]
        turn = [0]

        def load_raws(*srcs, parts=2):
            m = 4 // parts
            at = [(turn[0] + n) % 4 for n in range(len(srcs))]
            turn[0] += len(srcs)
            toks = [[] for _ in srcs]
            for h in range(parts):
                for n, (i, src) in enumerate(zip(at, srcs)):
                    toks[n].append(op("sync", f"d_raw{i}{h}", lambda e, h=h, i=i, src=src: e.dma_start(
                        raw[i][:, m * h:m * h + m, :], src[:, m * h:m * h + m, :]), *raw_free[i]))
            return list(zip(at, toks))

        def load_raw(src):
            return load_raws(src)[0]

        ctxs, xs = {}, {}
        r_wv, ctxs[0] = load_raws(kp(v_w), cv[0], parts=4)
        t_vec = op("scalar", "d_vec", lambda e: e.dma_start(cols[:, :], vecs))
        r_wk = load_raw(kp(k_w))
        xs[0] = load_raw(xv[0])

        def split_raw(r, hi, lo, he, le, *free):
            i, toks = r
            done = []
            for h in range(len(toks)):
                done += split_part(r, h, hi, lo, he[h % len(he)], le[h % len(le)], *free)
            return done

        def split_part(r, h, hi, lo, he, le, *free):
            i, toks = r
            m = 4 // len(toks)
            if h == 0:
                raw_free[i] = []
            rh, hh, lh = [v[:, m * h:m * h + m, :] for v in (raw[i], hi, lo)]
            if he == "scalar":
                th = op("scalar", "a_hi", lambda e: e.activation(hh, rh, ACT.Copy), toks[h], *free)
            else:
                th = op("vector", "v_hi", lambda e: e.tensor_copy(hh, rh), toks[h], *free)
            tl = op(le, "v_lo" if le == "vector" else "g_lo",
                    lambda e: e.tensor_tensor(lh, rh, hh.bitcast(F32), ALU.subtract), th, toks[h], *free)
            raw_free[i].append(tl)
            return [[th, tl]]

        bank_free = {i: [] for i in range(8)}

        def mm3(outp, a, b, first=True, last=True):
            def f(e):
                for n, (u, v) in enumerate(((a[0], b[0]), (a[1], b[0]), (a[0], b[1]))):
                    ins = e.matmul(outp, u, v, start=first and n == 0, stop=last and n == 2)
                return ins
            return f

        def mm_block(outp, a_of, b_of, ks=range(4)):
            def f(e):
                for k in ks:
                    ins = mm3(outp, a_of(k), b_of(k), first=k == 0, last=k == 3)(e)
                return ins
            return f

        def flat(toks):
            return [t for h in toks for t in h]

        ct_done, xt_done, v_done = {}, {}, {}
        ct_free, xt_free = {0: [], 1: []}, {0: [], 1: []}
        full = [R2[:, i, :] for i in range(4)]
        full_free = [[], [], [], []]
        nfull = [0]

        def norm_rs(slot, tok):
            for c in range(4):
                t = op("vector", "v_ag", lambda e, c=c: e.bn_aggr(mv[:, slot, c, :], st[:, c, :]), tok)
            t = op("vector", "v_ve", lambda e: e.tensor_scalar(
                ve[:, slot, :], mv[:, slot, :, 1], EPS, None, ALU.add), t)
            return op("gpsimd", "g_rs", lambda e: e.tensor_tensor(
                rs[:, slot, :], ve[:, slot, :], mh[:, :], ALU.pow), t, t_mh)

        def norm_one(src, slot, c, tok):
            return op("vector", "v_nm", lambda e: e.tensor_scalar(
                src[:, c, :], src[:, c, :], mv[:, slot, c, 0:1], rs[:, slot, c:c + 1],
                ALU.subtract, ALU.mult), tok)

        def turn_k(src, k, bk, *waits):
            def f(e):
                for c in range(4):
                    ins = e.transpose(bank(bk)[:, c * 128:(c + 1) * 128], src[:, c, k * 128:(k + 1) * 128], ident[:, :])
                return ins
            return op("tensor", "p_tr", f, t_id, *waits)

        def affine_split(k, bk, tt, w, b, hi, lo, fb, free):
            tf = op("vector", "v_fu", lambda e: e.tensor_scalar(
                fb, bank(bk), vec[:, w, k:k + 1], vec[:, b, k:k + 1], ALU.mult, ALU.add), tt, t_vec, *free)
            th = op("scalar", "a_xh", lambda e: e.activation(hi, fb, ACT.Copy), tf)
            tl = op("gpsimd", "g_xl", lambda e: e.tensor_tensor(lo, fb, hi.bitcast(F32), ALU.subtract), th)
            return tf, th, tl

        xn_done = {}

        def xn_part(b):
            i, toks = xs[b]
            for c in range(4):
                t = op("vector", "v_bn", lambda e, c=c: e.bn_stats(st[:, c, :], raw[i][:, c, :]), toks[c // 2])
            t = norm_rs(b % 2, t)
            for c in range(4):
                xn_done[b] = norm_one(raw[i], b % 2, c, t)

        def xt_part(b):
            i, _ = xs[b]
            done = []
            for k in range(4):
                tt = turn_k(raw[i], k, k, xn_done[b], *bank_free[k])
                n = nfull[0] % 4
                nfull[0] += 1
                tf, th, tl = affine_split(k, k, tt, 0, 1, XT[b % 2][0][:, k, :], XT[b % 2][1][:, k, :], full[n],
                                          full_free[n] + xt_free[b % 2])
                full_free[n] = [tl]
                bank_free[k] = [tf]
                done += [[th, tl]]
            raw_free[i] = [tt]
            xt_done[b] = [done[1], done[3]]

        kq_free = [[], [], [], []]
        nkq = [0]
        nbk = [0]
        sc_done = {}

        def proj_T(b, g, wt, w_done, acts, a_done, bias, scr, which):
            bk = next_bank()
            for h in range(2):
                tm = op("tensor", "p_pj", mm_block(
                    bank(bk), lambda k: [w[:, k, g * 128:(g + 1) * 128] for w in wt],
                    lambda k: [a[:, k, :] for a in acts], range(2 * h, 2 * h + 2)), *w_done[h], *a_done[h],
                    *(bank_free[bk] if h == 0 else []))
            n = nkq[0] % 4
            nkq[0] += 1
            dst = QK[n]
            th = op("scalar", "a_qh", lambda e: e.activation(
                dst[:, 0, :], bank(bk), ACT.Identity, bias=vec[:, bias, g:g + 1]), tm, t_vec, *kq_free[n])
            tl = op("vector", "v_ql", lambda e: e.scalar_tensor_tensor(
                out=dst[:, 1, :], in0=bank(bk), scalar=vec[:, bias, g:g + 1], in1=dst[:, 0, :].bitcast(F32),
                op0=ALU.add, op1=ALU.subtract), th, t_vec)
            bank_free[bk] = [tl]
            for h, tok in ((0, th), (1, tl)):
                td = op("sync", f"d_qk{n}", lambda e, h=h: e.dma_start(
                    scr[4 * b + g, h].rearrange("d j t -> j d t"), dst[:, h, :].bitcast(F32)), tok)
            kq_free[n] = [td]
            sc_done[(which, 4 * b + g)] = td
            return tm

        def proj_V(b, cs):
            bks = [next_bank() for _ in cs]
            parts = 4 if b == 0 else 2
            m = 4 // parts
            for h in range(parts):
                for c, bk in zip(cs, bks):
                    tm = op("tensor", "p_pj", mm_block(
                        bank(bk), lambda k, c=c: [a[:, k, c * 128:(c + 1) * 128] for a in CT[b % 2]],
                        lambda k: [w[:, k, :] for w in WV], range(m * h, m * h + m)),
                        *wv_done[h if b == 0 else 3], *ct_done[b][h],
                        *(bank_free[bk] if h == 0 else []))
                    if h == parts - 1:
                        tv = op("scalar", "a_v", lambda e, c=c, bk=bk: e.activation(
                            V[:, 4 * b + c, :], bank(bk), ACT.Copy), tm)
                        bank_free[bk] = [tv]
            v_done[b] = tv

        mm_banks = [4, 5, 6, 7]

        def next_bank():
            nbk[0] += 1
            return mm_banks[nbk[0] % len(mm_banks)]

        wv_done = []
        ct_done[0] = []
        for n in range(4):
            wv_done += split_part(r_wv, n, WV[0], WV[1], "vector", "vector")
            ct_done[0] += split_part(ctxs[0], n, CT[0][0], CT[0][1], "scalar", "vector")
        r_wq = load_raw(kp(q_w))
        wk_done = split_raw(r_wk, WKq[0], WKq[1], ["scalar"], ["gpsimd", "vector"])
        ctxs[1] = load_raw(cv[1])
        xn_part(0)
        m8 = R2[0:4, 0, 0:128].bitcast(U8)
        mf = R2[0:4, 1, :]
        t_m8 = op("sync", "d_m8", lambda e: e.dma_start(m8, mask))
        t = op("vector", "v_mf", lambda e: e.tensor_scalar(mf, m8, 1.0, None, ALU.subtract), t_m8)
        t = op("vector", "v_mf", lambda e: e.tensor_scalar(mf, mf, 2.0 ** 127, None, ALU.mult), t)
        t_mk = op("sync", "d_mk", lambda e: e.dma_start(mk, mf), t)
        t_on = op("sync", "d_on", lambda e: e.dma_start(on.rearrange("a (p c) -> (a p) c", c=32), ones[0:16, :]), t_ones)
        t_cb = op("sync", "d_cb", lambda e: e.dma_start(cbt[:, :], c_b.partition_broadcast(128)))
        full_free[0] = [t_mk]
        full_free[1] = [t_mk]
        wq_done = split_raw(r_wq, WKq[2], WKq[3], ["vector", "scalar"], ["gpsimd"])
        xs[1] = load_raw(xv[1])

        stk_free, stk_done = {}, {}

        def load_stack(s):
            n = s % 3
            Q_, K_ = STK[n]
            both = lambda scr: scr[s].rearrange("h d j t -> (h d) j t")
            w = [sc_done[("q", s)], sc_done[("k", s)], t_mk, *stk_free[n]]
            qd, kd = Q_.bitcast(F32), K_.bitcast(F32)
            if s < 3:
                for row in (qd[96:97], kd[97:98]):
                    op("sync", f"d_st{n}", lambda e, row=row: e.dma_start(
                        row, on.rearrange("(o a) t -> o a t", a=1).broadcast_to([1, 4, 512])), t_on, *stk_free[n])
            for d, src in ((qd[0:64], both(qs)), (kd[32:96], both(ks)), (qd[64:96], qs[s, 0]), (kd[0:32], ks[s, 0]),
                           (kd[96:97], mk[s // 4:s // 4 + 1].rearrange("o (a t) -> o a t", a=1).broadcast_to([1, 4, 512]))):
                t = op("sync", f"d_st{n}", lambda e, d=d, src=src: e.dma_start(d, src), *w)
            stk_done[s] = t

        maxes = [(s, n) for s in range(NS) for n in range(16)]
        nm = [0]

        def next_max():
            if nm[0] < len(maxes):
                s, n = maxes[nm[0]]
                nm[0] += 1
                max_head(s, n)
                if n == 15:
                    return s
            return None

        nu = [0]
        ring = []

        def next_ring():
            nu[0] += 1
            return ring[nu[0] % len(ring)]

        late = []

        mx_free = [[], []]
        mx_part = {}
        m_done = {}

        def max_head(s, n):
            qc, j = n // 4, n % 4
            bk = next_ring()
            Q_, K_ = STK[s % 3]
            tm = op("tensor", "p_s1", lambda e: e.matmul(
                bank(bk), Q_[0:97, j, qc * 128:(qc + 1) * 128], K_[0:97, j, :], start=True, stop=True),
                stk_done[s], *bank_free[bk])
            tv = op("vector", "v_mx", lambda e: e.tensor_reduce(
                mx[:, s % 2, 4 * j + qc:4 * j + qc + 1], bank(bk), AX.X, ALU.max), tm, *mx_free[s % 2])
            bank_free[bk] = [tv]
            mx_part[s] = tv

        mt_free = []

        def max_rows(s):
            bk = next_ring()
            tp = op("tensor", "p_mt", lambda e: e.transpose(bank(bk)[0:16, 0:128], mx[:, s % 2, :], ident[:, :]),
                    mx_part[s], t_id, *bank_free[bk])
            mx_free[s % 2] = [tp]
            ta = op("scalar", "a_mt", lambda e: e.activation(
                mT[:, :], bank(bk)[0:16, 0:128], ACT.Copy, scale=-1.0), tp, *mt_free)
            bank_free[bk] = [ta]
            q97 = STK[s % 3][0].bitcast(F32)[97:98, :, :]
            td = op("sync", "d_m", lambda e: e.dma_start(q97, mT[:, :].bitcast(F32)), ta)
            mt_free[:] = [td]
            m_done[s] = td

        for b in range(B):
            if b == B - 1:
                stk_free[1] = xt_free[0]
                load_stack(1)
                ring[:] = [0, 1, 2, 3]
            if b == 0:
                proj_V(b, range(4))
                ct_done[0] = ct_done[0][2:]
            elif b < B - 1:
                proj_V(b, range(2))
                proj_V(b, range(2, 4))
            else:
                for c in range(4):
                    proj_V(b, [c])
                    next_max(), next_max()
            if b + 1 < B and b > 0:
                xn_part(b + 1)
            for g in range(4):
                if b == 0 and g == 2:
                    xt_part(0)
                    xn_part(1)
                tm = proj_T(b, g, WKq[0:2], wk_done, CT[b % 2], ct_done[b], 3, ks, "k")
                if b == B - 1:
                    next_max(), next_max()
            ct_free[b % 2] = [tm]
            if b == B - 2:
                stk_free[0] = ct_free[0]
                load_stack(0)
            if b + 1 < B:
                ct_done[b + 1] = split_raw(ctxs[b + 1], CT[(b + 1) % 2][0], CT[(b + 1) % 2][1], ["scalar"],
                                           ["gpsimd"], *ct_free[(b + 1) % 2])
                if b + 2 < B:
                    ctxs[b + 2] = load_raw(cv[b + 2])
                if b > 0:
                    xt_part(b + 1)
                    if b + 2 < B:
                        xs[b + 2] = load_raw(xv[b + 2])
            if b == B - 1:
                ring[:] = [0, 1, 2, 3, 4, 5]
                mm_banks[:] = [6, 7]
                stk_free[2] = ct_free[1]
                load_stack(2)
            for g in range(4):
                if b == B - 1 and g == 2:
                    max_rows(0)
                tm = proj_T(b, g, WKq[2:4], wq_done, XT[b % 2], xt_done[b], 2, qs, "q")
                if b == 0 and g == 1:
                    xt_part(1)
                    xs[2] = load_raw(xv[2])
                if b == B - 1:
                    next_max(), next_max()
            xt_free[b % 2] = [tm]
        t_p0 = tm

        p_done, p_read = {}, {i: [] for i in range(6)}

        def exp_head(s, kc, j):
            bk = next_ring()
            Q_, K_ = STK[s % 3]
            tm = op("tensor", "p_s2", lambda e: e.matmul(
                bank(bk), K_[0:98, j, kc * 128:(kc + 1) * 128], Q_[0:98, j, :], start=True, stop=True),
                stk_done[s], m_done[s], *bank_free[bk])
            r = (2 * (4 * s + kc) + j // 2) % 6
            ta = op("scalar", "a_ex", lambda e: e.activation(Pt[:, r, j % 2, :], bank(bk), ACT.Exp, scale=SCALE),
                    tm, t_p0, *p_read[r])
            bank_free[bk] = [ta]
            if j % 2:
                p_read[r] = []
                p_done[(s, kc, j // 2)] = ta
            stk_free[s % 3] = [tm]

        acc_done, acc_free = {}, [[], []]

        def add_unit(s, kc, hp, eng):
            r = (2 * (4 * s + kc) + hp) % 6
            a, c = Pt[:, (r - 2) % 6, :, :], Pt[:, r, :, :]
            t = op(eng, "g_ac" if eng == "gpsimd" else "v_ac", lambda e: e.tensor_tensor(R0[:, 2 * hp:2 * hp + 2, :], a, c, ALU.add),
                   p_done[(s, kc, hp)], p_done[(s, kc - 1, hp)], *acc_free[hp])
            acc_done[(s, kc, hp)] = t
            p_read[r].append(t)
            p_read[(r - 2) % 6].append(t)

        pv_done = {}

        def pv(s, kc):
            b, g = divmod(s, 4)

            def f(e):
                for j in range(4):
                    r = (2 * (4 * s + kc) + j // 2) % 6
                    c = (4 * g + j) * 32
                    ins = e.matmul(bank(6)[32 * j:32 * j + 32, :], V[:, 4 * b + kc, c:c + 32], Pt[:, r, j % 2, :],
                                   start=kc == 0, stop=kc == 3)
                return ins
            w = list(bank_free[6]) if kc == 0 else []
            t = op("tensor", "p_pv", f, p_done[(s, kc, 0)], p_done[(s, kc, 1)], v_done[b], *w)
            for hp in range(2):
                p_read[(2 * (4 * s + kc) + hp) % 6].append(t)
            if kc == 3:
                ta = op("scalar", "a_pv", lambda e: e.activation(R1[:, 0, :], bank(6), ACT.Copy), t, *att_free)
                bank_free[6] = [ta]
                pv_done[s] = ta

        att_free = []
        at_free = []
        t1_free = []
        at_done = {}

        at_tok = {}

        def sums(s, kc):
            def f(e):
                for j in range(4):
                    ins = e.matmul(bank(7)[32 * j:32 * j + 32, :], ones[:, :], R0[:, j, :], start=kc == 1, stop=kc == 3)
                return ins
            ts = op("tensor", "p_sm", f, acc_done[(s, kc, 0)], acc_done[(s, kc, 1)], t_ones,
                    *(bank_free[7] if kc == 1 else []))
            acc_free[0], acc_free[1] = [ts], [ts]
            at_tok[s] = ts

        def divide_a(s):
            t = op("vector", "v_t1", lambda e: e.transpose(R1[:, 1, :], bank(7)), at_tok[s])
            bank_free[7] = [t]
            at_tok[s] = t

        def divide_b(s):
            t = op("vector", "v_rc", lambda e: e.reciprocal(rc[:, :], R1[:, 1, 0:512:32]), at_tok[s])
            at_tok[s] = op("vector", "v_t2", lambda e: e.transpose(
                R1[:, 2, :].rearrange("p (a b) -> p a b", b=32),
                rc[:, :].rearrange("p (a o) -> p a o", o=1).broadcast_to([128, 16, 32])), t)

        def divide_c(s):
            tm = op("vector", "v_at", lambda e: e.tensor_tensor(R1[:, 3, :], R1[:, 0, :], R1[:, 2, :], ALU.mult),
                    at_tok[s], pv_done[s], *t1_free)
            att_free[:] = [tm]
            at_tok[s] = tm

        def split_out(s):
            g = s % 4
            w = list(at_free) if g == 0 else []
            ta = R1[:, 3, :]
            t = op("scalar", "a_ab", lambda e: e.activation(ta, ta, ACT.Identity, bias=vec[:, 4, g:g + 1]), at_tok[s])
            th = op("scalar", "a_ah", lambda e: e.activation(AT[0][:, g, :], ta, ACT.Copy), t, *w)
            tl = op("gpsimd", "g_al", lambda e: e.tensor_tensor(
                AT[1][:, g, :], ta, AT[0][:, g, :].bitcast(F32), ALU.subtract), th, t)
            t1_free[:] = [tl]
            at_done[s] = [th, tl]

        hd_done = {}
        xr_free = [list(full_free[i]) for i in range(4)]

        def x_load(b):
            return [op("sync", f"d_xr{c}", lambda e, c=c: e.dma_start(R2[:, c, :], xv[b][:, c, :]), *xr_free[c])
                    for c in range(4)]

        def x_plus_bias(toks, c):
            toks[c] = op("gpsimd", "g_xc", lambda e: e.tensor_tensor(
                R2[:, c, :], R2[:, c, :], cbt[:, :], ALU.add), toks[c], t_cb)

        def cproj_tile(b, c, toks, outp, *waits):
            tm = op("tensor", "p_cp", mm_block(
                outp, lambda k: [a[:, k, c * 128:(c + 1) * 128] for a in AT], lambda k: [w[:, k, :] for w in WC]),
                *wc_done, *at_done[4 * b + 3], *at_done[4 * b + 2], *waits)
            tv = op("vector", "v_hd", lambda e: e.tensor_tensor(R2[:, c, :], outp, R2[:, c, :], ALU.add), tm, toks[c])
            td = op("sync", f"d_hd{c}", lambda e: e.dma_start(hd[4 * b + c], R2[:, c, :]), tv)
            xr_free[c] = [td]
            hd_done[4 * b + c] = td
            at_free[:] = [tm]
            return tv

        def cproj(b, c, toks):
            bk = next_ring()
            bank_free[bk] = [cproj_tile(b, c, toks, bank(bk), *bank_free[bk])]

        ti = op("sync", "d_wc", lambda e: e.dma_start(R2[:, :, :], kp(c_w)), *[t for f in full_free for t in f])
        wfree = [f[0] for f in kq_free]
        wc_done = []

        def split_wc(k):
            th = op("scalar", "a_wc", lambda e: e.activation(WC[0][:, k, :], R2[:, k, :], ACT.Copy), ti, *wfree)
            tl = op("vector", "v_wc", lambda e: e.tensor_tensor(
                WC[1][:, k, :], R2[:, k, :], WC[0][:, k, :].bitcast(F32), ALU.subtract), th)
            wc_done.append(tl)
            xr_free[k] = [tl]

        acc_free[0], acc_free[1] = list(raw_free[2]), list(raw_free[2])
        att_free[:] = list(raw_free[3])
        at_free[:] = list(xt_free[1])

        rw_free = [[("p_pv", 0)], [("p_pv", 0)]]
        nslab = [0]
        slab_done = {}

        slab_raw = {}

        def load_slab(f):
            n = nslab[0] % 2
            nslab[0] += 1
            op("sync", f"d_w{n}", lambda e: e.dma_start(
                RW[:, n, 0:512].rearrange("p (k n) -> p k n", k=4), kp(fc_w)[:, :, f * 128:(f + 1) * 128]), *rw_free[n])
            t = op("sync", f"d_w{n}", lambda e: e.dma_start(RW[:, n, 512:1024], pj_w[f * 128:(f + 1) * 128, :]),
                   *rw_free[n])
            slab_raw[f] = (n, t)

        def split_slab(f, *waits, le="gpsimd"):
            n, t = slab_raw[f]
            sl = slab(f)
            done = []
            for i in range(2):
                src = RW[:, n, 512 * i:512 * i + 512]
                th = op("vector", "v_sh", lambda e, i=i, src=src: e.tensor_copy(sl[2 * i], src), t, *waits)
                tl = op(le, "g_sl" if le == "gpsimd" else "v_sl", lambda e, i=i, src=src: e.tensor_tensor(
                    sl[2 * i + 1], src, sl[2 * i].bitcast(F32), ALU.subtract), th)
                done += [th, tl]
            rw_free[n] = [done[3]]
            slab_done[f] = [done[2], done[3]]

        LN = [HN, R0, R0, R0]
        ln_free = {}
        ln_tok = {}
        yt_done, yt_free = {}, [raw_free[0] + raw_free[1], []]
        fu_free = [[], []]

        def ln2_load(b):
            for c in range(4):
                ln_tok[(b, c)] = op("sync", f"d_h{c}", lambda e, c=c: e.dma_start(LN[b][:, c, :], hd[4 * b + c]),
                                    hd_done[4 * b + c], *ln_free[b])

        def ln2_bn(b, c):
            ln_tok[(b, "bn")] = op("vector", "v_bn", lambda e: e.bn_stats(st[:, c, :], LN[b][:, c, :]), ln_tok[(b, c)])

        def ln2_rs(b):
            ln_tok[(b, "rs")] = norm_rs(b % 2, ln_tok[(b, "bn")])

        def ln2_norm(b, c):
            ln_tok[(b, "nm")] = norm_one(LN[b], b % 2, c, ln_tok[(b, "rs")])

        def yt_k(b, k, bk=None):
            Y = YT[b % 2]
            if bk is None:
                bk = next_ring()
            tt = turn_k(LN[b], k, bk, ln_tok[(b, "nm")], *bank_free[bk])
            n = k % 2
            tf, th, tl = affine_split(k, bk, tt, 5, 6, Y[:, 0, k, :], Y[:, 1, k, :], FU[:, n, :],
                                      fu_free[n] + yt_free[b % 2])
            bank_free[bk] = [tf]
            fu_free[n] = [tl]
            yt_done[b] = [th, tl]
            ln_free[b + 1] = [tt]

        h_done = {}
        h_free = [[], []]
        g_free = {}
        hb_done = {}

        def fc(i):
            b, f = divmod(i, NF)
            bk = 4 + i % 2
            sl = slab(f)
            Y = YT[b % 2]
            tm = op("tensor", "p_fc", mm_block(
                bank(bk), lambda k: [sl[s][:, k * 128:(k + 1) * 128] for s in range(2)],
                lambda k: [Y[:, s, k, :] for s in range(2)]),
                *slab_done[f], *yt_done[b], *bank_free[bk])
            if f == NF - 1:
                yt_free[b % 2] = [tm]
            n = i % 2
            early = i < 12
            g = HN[:, n, :] if early else R1[:, n, :]
            tg = op("scalar", "a_g", lambda e: e.activation(
                g, bank(bk), ACT.Gelu_apprx_tanh, bias=fcb[:, f:f + 1]), tm, *g_free[(early, n)])
            bank_free[bk] = [tg]
            th = op("vector", "v_hh", lambda e: e.tensor_copy(HR[:, n, 0, :], g), tg, *h_free[n])
            tl = op("vector", "v_hl", lambda e: e.tensor_tensor(
                HR[:, n, 1, :], g, HR[:, n, 0, :].bitcast(F32), ALU.subtract), th)
            g_free[(early, n)] = [tl]
            h_done[i] = [tl]

        def pj(i):
            b, f = divmod(i, NF)
            n = i % 2
            sl = slab(f)
            for c in range(4):
                tm = op("tensor", "p_pr", mm3(
                    bank(c), [HR[:, n, s, c * 128:(c + 1) * 128] for s in range(2)], [sl[2], sl[3]],
                    first=f == 0, last=f == NF - 1), *h_done[i], *(bank_free[c] if f == 0 else []))
                if f == NF - 1:
                    to = op("vector", "v_o", lambda e, c=c: e.tensor_tensor(
                        R2[:, c, :], bank(c), R2[:, c, :], ALU.add), tm, hb_done[(b, c)])
                    bank_free[c] = [to]
                    xr_free[c] = [op("sync", f"d_o{c}", lambda e, c=c: e.dma_start(ov[4 * b + c], R2[:, c, :]), to)]
            h_free[n] = [tm]

        NI = 4 * NS
        SLABS = (52, 53, 56, 59)

        def max_next(s, kc):
            r = next_max() if nm[0] < 16 * (s + 2) or kc >= 2 else None
            late[:] = [(q, n - 1) for q, n in late]
            if late and late[0][1] == 0:
                max_rows(late.pop(0)[0])
            if r is not None:
                late.append((r, 4))

        xtoks = {}
        for i in range(NI):
            s, kc = divmod(i, 4)
            b = i // 16
            if kc == 0 and s >= 1 and s + 2 < NS:
                load_stack(s + 2)
            divided = i >= 5 and kc >= 2
            exp_head(s, kc, 0)
            exp_head(s, kc, 1)
            max_next(s, kc)
            max_next(s, kc)
            if divided:
                (divide_a if kc == 2 else divide_c)(s - 1)
            exp_head(s, kc, 2)
            max_next(s, kc)
            if kc == 1 and i >= 5:
                sums(s - 1, 3)
            if i >= 20 and 5 <= i % 16 < 9:
                cproj(b - 1, i % 16 - 5, xtoks[b - 1])
            exp_head(s, kc, 3)
            max_next(s, kc)
            if divided and kc == 2:
                divide_b(s - 1)
            if kc == 3:
                sums(s, 1)
            if kc % 2:
                add_unit(s, kc, 0, "gpsimd")
                add_unit(s, kc, 1, "vector" if i >= 54 else "gpsimd")
            if i >= 5 and kc == 3 and (s - 1) % 4:
                split_out(s - 1)
            if i >= 5 and kc == 0 and (s - 2) % 4 == 0:
                split_out(s - 2)
            if i >= 1:
                pv(*divmod(i - 1, 4))
            if i in (40, 44, 48, 52):
                yt_k(0, (i - 40) // 4)
            if 1 <= i <= 4:
                split_wc(i - 1)
            if i % 16 == 8:
                xtoks[b] = x_load(b)
            if 10 <= i % 16 < 14:
                x_plus_bias(xtoks[b], i % 16 - 10)
            if i == 24:
                ln_free[0] = [t_p0]
                ln2_load(0)
            if 26 <= i < 30:
                ln2_bn(0, i - 26)
            if i == 30:
                ln2_rs(0)
            if 31 <= i < 39 and i % 2:
                ln2_norm(0, (i - 31) // 2)
            if i == 48:
                rw_free = [[("p_pv", counts["p_pv"])]] * 2
                load_slab(0)
                load_slab(1)
            if i in SLABS:
                f = SLABS.index(i)
                split_slab(f, t_p0 if f < 2 else t_s13, le="gpsimd" if f < 2 else "vector")
                load_slab(f + 2)
            if i == 55:
                t_s13 = ("p_s2", counts["p_s2"])
        t_s15 = ("p_s2", counts["p_s2"])
        sums_read = [acc_done[(NS - 1, 3, hp)] for hp in range(2)]
        pv(NS - 1, 3)
        t_v = ("p_pv", counts["p_pv"])
        yt_free[1] = [t_v]
        h_free = [[t_v], [t_v]]
        g_free = {(True, n): list(ln_free[1]) for n in range(2)}
        t_pb = op("sync", "d_pb", lambda e: e.dma_start(cbt[:, :], pj_b.partition_broadcast(128)),
                  *xtoks[3])
        split_slab(4, t_s15, le="vector")
        load_slab(6)
        split_slab(5, t_s15)

        NJ = B * NF
        for i in range(NJ + 1):
            b, f = divmod(i, NF)
            if i < NJ:
                fc(i)
            if i == 0:
                sums(NS - 1, 3)
                divide_a(NS - 1)
                divide_b(NS - 1)
                divide_c(NS - 1)
                split_out(NS - 1)
                g_free[(False, 0)] = g_free[(False, 1)] = [att_free[0]]
                ln_free[1] = [("p_sm", counts["p_sm"])]
            if i >= 1:
                pj(i - 1)
            if 2 <= i < 6:
                bk = 6 + i % 2
                bank_free[bk] = [cproj_tile(3, i - 2, xtoks[3], bank(bk), *bank_free[bk])]
            if 1 <= i < 9:
                load_slab(i + 6)
                split_slab(i + 5, t_v, *sums_read, *([("p_cp", counts["p_cp"])] if i >= 6 else []))
            if i == 9:
                load_slab(15)
                split_slab(14, ("p_cp", counts["p_cp"]))
            if i == 13:
                split_slab(15, *g_free[(True, 0)], *g_free[(True, 1)])
            if i < NJ:
                if f == (8 if b == 0 else 3):
                    for c in range(4):
                        t = op("sync", f"d_hb{c}", lambda e, c=c, b=b: e.dma_start(R2[:, c, :], hd[4 * b + c]),
                               *xr_free[c])
                        hb_done[(b, c)] = op("gpsimd", "g_hb", lambda e, c=c: e.tensor_tensor(
                            R2[:, c, :], R2[:, c, :], cbt[:, :], ALU.add), t, t_pb)
                if b + 1 < B:
                    if f == 2:
                        ln2_load(b + 1)
                    if 3 <= f < 7:
                        ln2_bn(b + 1, f - 3)
                    if f == 6:
                        ln2_rs(b + 1)
                    if 7 <= f < 11:
                        ln2_norm(b + 1, f - 7)
                    if 11 <= f < 15:
                        yt_k(b + 1, f - 11, 6 + f % 2)
        for c in range(4):
            progs["sync"].append((None, list(xr_free[c]), None))

        def flush_all(name, eng):
            tail = [p for p in progs[name] if p[0] is None]
            progs[name] = [p for p in progs[name] if p[0] is not None]
            flush(name, eng)
            for _, waits, _ in tail:
                for s, v in waits:
                    eng.wait_ge(sems[s], v)

        block = ctx.enter_context(nc.Block())

        @block.sync
        def _(eng):
            flush_all("sync", eng)

        @block.scalar
        def _(eng):
            flush_all("scalar", eng)

        @block.gpsimd
        def _(eng):
            flush_all("gpsimd", eng)

        @block.vector
        def _(eng):
            flush_all("vector", eng)

        @block.tensor
        def _(eng):
            flush_all("tensor", eng)


_PRE = "L0_xattn_"
_COLS = ["ln1_w", "ln1_b", "q_b", "k_b", "v_b", "ln2_w", "ln2_b", "fc_b"]
_REST = ["q_w", "k_w", "v_w", "cproj_w", "cproj_b", "fc_w", "proj_w", "proj_b"]


def kernel(**inputs):
    import numpy as _np
    import concourse.bacc as _bacc
    from concourse import mybir as _mybir
    from concourse.bass_utils import run_bass_kernel_spmd as _run

    nc = _bacc.Bacc("TRN2", target_bir_lowering=False, num_devices=1)
    data = {"x": _np.asarray(inputs["x"]),
            "ctxT": _np.asarray(inputs["ctx_2048"]).transpose(0, 2, 1),
            "mask": _np.asarray(inputs["mask_BxS2_bf1"]).view(_np.uint8)}
    data["vecs"] = _np.concatenate([_np.asarray(inputs[_PRE + n]).reshape(-1, 128).T for n in _COLS], axis=1)
    for n in _REST:
        data[n] = _np.asarray(inputs[_PRE + n])
    arrays, args = {}, []
    for n, a in data.items():
        a = _np.ascontiguousarray(a)
        arrays[f"in_{n}"] = a
        args.append(nc.dram_tensor(f"in_{n}", a.shape, _mybir.dt.from_np(a.dtype), kind="ExternalInput").ap())
    args.append(nc.dram_tensor("out_0", (4, 512, 512), _mybir.dt.float32, kind="ExternalOutput").ap())
    cross_attention_block(nc, *args)
    r = _run(nc, [arrays], core_ids=[0])
    return r.results[0]["out_0"]
```
